# Optimizing a Trainium2 kernel written in Bass

```python
import numpy as np
import jax
import jax.numpy as jnp

def _softmax(x, axis=-1):
    return jax.nn.softmax(x, axis=axis)

def _gelu(x):
    return jax.nn.gelu(x, approximate=True)

def _silu(x):
    return jax.nn.silu(x)

def _sigmoid(x):
    return jax.nn.sigmoid(x)

def _layernorm(x, axis=-1, eps=1e-05):
    m = jnp.mean(x, axis=axis, keepdims=True)
    v = jnp.var(x, axis=axis, keepdims=True)
    return (x - m) / jnp.sqrt(v + eps)

def _scatter_add(tgt, idx, src, axis=0):
    return tgt.at[idx].add(src)

def _segment_sum(src, seg, n):
    return jax.ops.segment_sum(src, seg, n)
kernel_name = 'mk_macaron_d1_jaxref_r4_9c28f5'

def setup_inputs(seed: int=0):
    np.random.seed(seed)
    _w = jnp.asarray

    def _L0_attn_setup():
        import jax, jax.numpy as jnp
        import numpy as np
        E = 256
        HID = 256
        H = 16
        D = HID // H
        ROPE_BASE = 10000.0

        def _rope(t):
            S = t.shape[2]
            inv_freq = 1.0 / ROPE_BASE ** (jnp.arange(0, D, 2, dtype=jnp.float32) / D)
            ang = jnp.arange(S, dtype=jnp.float32)[:, None] * inv_freq[None, :]
            cos, sin = (jnp.cos(ang), jnp.sin(ang))
            t1, t2 = (t[..., 0::2], t[..., 1::2])
            r1 = t1 * cos - t2 * sin
            r2 = t1 * sin + t2 * cos
            return jnp.stack([r1, r2], axis=-1).reshape(t.shape).astype(t.dtype)
        key = jax.random.key(seed)
        ks = jax.random.split(key, 7)
        sc_in = 1.0 / np.sqrt(E)
        sc_hid = 1.0 / np.sqrt(HID)
        return {'x': jax.random.normal(ks[0], (2, 512, E), dtype=jnp.float32), 'Wq': jax.random.normal(ks[1], (HID, E), dtype=jnp.float32) * sc_in, 'Wk': jax.random.normal(ks[2], (HID, E), dtype=jnp.float32) * sc_in, 'Wv': jax.random.normal(ks[3], (HID, E), dtype=jnp.float32) * sc_in, 'bv': jax.random.normal(ks[4], (HID,), dtype=jnp.float32) * sc_in, 'Wo': jax.random.normal(ks[5], (E, HID), dtype=jnp.float32) * sc_hid, 'bo': jax.random.normal(ks[6], (E,), dtype=jnp.float32) * sc_hid}
    _L0_attn_in = _L0_attn_setup()

    def _L0_ffn_setup():
        import jax, jax.numpy as jnp
        import numpy as np
        import math
        BETA = 0.9
        THRESHOLD = 1.0
        NUM_STEPS = 5
        ALPHA = 2.0

        @jax.custom_vjp
        def spike_fn(u):
            return (u > 0).astype(u.dtype)

        def _spike_fwd(u):
            return (spike_fn(u), u)

        def _spike_bwd(u, g):
            s = jnp.pi / 2.0 * ALPHA * u
            return (g * (ALPHA / 2.0) / (1.0 + s * s),)
        spike_fn.defvjp(_spike_fwd, _spike_bwd)
        key = jax.random.key(seed)
        k1, k2, k3 = jax.random.split(key, 3)
        n_embd = 256
        x = jax.random.normal(k1, (4, 512, n_embd), dtype=jnp.float32)
        W_fc = jax.random.normal(k2, (4 * n_embd, n_embd), dtype=jnp.float32) / math.sqrt(n_embd)
        W_proj = jax.random.normal(k3, (n_embd, 4 * n_embd), dtype=jnp.float32) / math.sqrt(4 * n_embd)
        return {'x': x, 'W_fc': W_fc, 'W_proj': W_proj}
    _L0_ffn_in = _L0_ffn_setup()
    _d = {'L0_attn_x': _L0_attn_in['x'], 'L0_attn_Wq': _L0_attn_in['Wq'], 'L0_attn_Wk': _L0_attn_in['Wk'], 'L0_attn_Wv': _L0_attn_in['Wv'], 'L0_attn_bv': _L0_attn_in['bv'], 'L0_attn_Wo': _L0_attn_in['Wo'], 'L0_attn_bo': _L0_attn_in['bo'], 'L0_ffn_W_fc': _L0_ffn_in['W_fc'], 'L0_ffn_W_proj': _L0_ffn_in['W_proj']}
    _x0 = _d['L0_attn_x']
    _d['L0_attn_x'] = jax.random.normal(jax.random.fold_in(jax.random.key(seed), 1), (2, 2048, 256), dtype=_x0.dtype)
    del _x0
    return _d

def reference(L0_attn_x, L0_attn_Wq, L0_attn_Wk, L0_attn_Wv, L0_attn_bv, L0_attn_Wo, L0_attn_bo, L0_ffn_W_fc, L0_ffn_W_proj):

    def _L0_attn_ref(x, Wq, Wk, Wv, bv, Wo, bo):
        import jax, jax.numpy as jnp
        import numpy as np
        E = 256
        HID = 256
        H = 16
        D = HID // H
        ROPE_BASE = 10000.0

        def _rope(t):
            S = t.shape[2]
            inv_freq = 1.0 / ROPE_BASE ** (jnp.arange(0, D, 2, dtype=jnp.float32) / D)
            ang = jnp.arange(S, dtype=jnp.float32)[:, None] * inv_freq[None, :]
            cos, sin = (jnp.cos(ang), jnp.sin(ang))
            t1, t2 = (t[..., 0::2], t[..., 1::2])
            r1 = t1 * cos - t2 * sin
            r2 = t1 * sin + t2 * cos
            return jnp.stack([r1, r2], axis=-1).reshape(t.shape).astype(t.dtype)
        B, S, _ = x.shape
        scale = 1.0 / np.sqrt(D)
        q = jnp.einsum('bse,he->bsh', x, Wq).reshape(B, S, H, D).transpose(0, 2, 1, 3)
        k = jnp.einsum('bse,he->bsh', x, Wk).reshape(B, S, H, D).transpose(0, 2, 1, 3)
        v = (jnp.einsum('bse,he->bsh', x, Wv) + bv).reshape(B, S, H, D).transpose(0, 2, 1, 3)
        q = _rope(q)
        k = _rope(k)
        scores = jnp.einsum('bhsd,bhtd->bhst', q, k) * scale
        causal = jnp.triu(jnp.ones((S, S), dtype=bool), k=1)
        scores = jnp.where(causal, -jnp.inf, scores)
        probs = jax.nn.softmax(scores, axis=-1)
        out = jnp.einsum('bhst,bhtd->bhsd', probs, v)
        out = out.transpose(0, 2, 1, 3).reshape(B, S, HID)
        return jnp.einsum('bsh,eh->bse', out, Wo) + bo

    def _L0_ffn_ref(x, W_fc, W_proj):
        import jax, jax.numpy as jnp
        import numpy as np
        import math
        BETA = 0.9
        THRESHOLD = 1.0
        NUM_STEPS = 5
        ALPHA = 2.0

        @jax.custom_vjp
        def spike_fn(u):
            return (u > 0).astype(u.dtype)

        def _spike_fwd(u):
            return (spike_fn(u), u)

        def _spike_bwd(u, g):
            s = jnp.pi / 2.0 * ALPHA * u
            return (g * (ALPHA / 2.0) / (1.0 + s * s),)
        spike_fn.defvjp(_spike_fwd, _spike_bwd)
        h = jnp.square(jax.nn.relu(jnp.einsum('bsd,fd->bsf', x, W_fc)))
        y = jnp.einsum('bsf,df->bsd', h, W_proj)

        def step(mem, _):
            reset = jax.lax.stop_gradient(spike_fn(mem - THRESHOLD))
            mem_new = BETA * mem + y - reset * THRESHOLD
            spk = spike_fn(mem_new - THRESHOLD)
            return (mem_new, spk)
        mem0 = jnp.zeros_like(y)
        _, spks = jax.lax.scan(step, mem0, None, length=NUM_STEPS)
        return jnp.sum(spks, axis=0) / NUM_STEPS
    x = L0_attn_x
    x = x + 0.5 * _L0_ffn_ref(_layernorm(x, axis=-1), L0_ffn_W_fc, L0_ffn_W_proj)
    x = x + _L0_attn_ref(_layernorm(x, axis=-1), L0_attn_Wq, L0_attn_Wk, L0_attn_Wv, L0_attn_bv, L0_attn_Wo, L0_attn_bo)
    x = x + 0.5 * _L0_ffn_ref(_layernorm(x, axis=-1), L0_ffn_W_fc, L0_ffn_W_proj)
    return x

_drawn_inputs = setup_inputs


def setup_inputs(seed=0):
    import zlib

    import numpy as np

    out = dict(_drawn_inputs(seed))
    spreads = {}
    factors = {}
    for name, (base, spread) in spreads.items():
        noise = np.random.default_rng([zlib.crc32(name.encode()), seed]).standard_normal(out[name].shape)
        drawn = base * np.exp(spread * noise) if base else spread * noise
        out[name] = jnp.asarray(drawn.astype(out[name].dtype))
    for name, factor in factors.items():
        out[name] = (out[name] * factor).astype(out[name].dtype)
    return out
```

```python
import concourse.bass as bass
from concourse import mybir
from contextlib import ExitStack

F32 = mybir.dt.float32
F32R = mybir.dt.float32r
BF16 = mybir.dt.bfloat16
ALU = mybir.AluOpType
ACT = mybir.ActivationFunctionType
AX = mybir.AxisListType

P = 128
E = 256
EC = E // P
F = 1024
FC = F // P
B = 2
S = 2048
TOK = B * S
CH = 512
T = CH // P
NC = TOK // CH
H = 16
D = 16
G = 4
NG = H // G
EPS = 1e-5
BETA = 0.9
THRESHOLD = 1.0
STEPS = 5
HB = 3
LAG = 2
QS, KS = (0, 0, 1, 1, 0, 2), (0, 1, 0, 1, 2, 0)
NT = len(QS)
KR = NT * D
KC = KR + 3
NEG = -3.0e38


def ffn_phase(nc, first, src, dst, w, io):
    tag = "a" if first else "c"
    with ExitStack() as ctx:
        def sb(name, shape, dt=F32):
            return ctx.enter_context(nc.sbuf_tensor(f"{name}_{tag}", shape, dt))

        def pb(name, shape, dt=F32):
            return ctx.enter_context(nc.psum_tensor(f"{name}_{tag}", shape, dt))

        def sem(name):
            return ctx.enter_context(nc.semaphore(f"{name}_{tag}"))

        PN = 3 * E if first else E
        up_hi, up_lo = sb("up_hi", [P, EC, F], F32R), sb("up_lo", [P, EC, F], F32R)
        down_hi, down_lo = sb("down_hi", [P, FC, E], F32R), sb("down_lo", [P, FC, E], F32R)
        proj_hi, proj_lo = sb("proj_hi", [P, EC, PN], F32R), sb("proj_lo", [P, EC, PN], F32R)
        ident, identb = sb("ident", [P, P]), sb("identb", [P, P], BF16)
        bias = sb("bias", [P, E])

        xin = sb("xin", [P, T, E])
        xn = sb("xn", [P, T, E])
        xT_hi, xT_lo = sb("xT_hi", [P, EC, CH], F32R), sb("xT_lo", [P, EC, CH], F32R)
        mT_hi, mT_lo = sb("mT_hi", [P, EC, CH], F32R), sb("mT_lo", [P, EC, CH], F32R)
        stats, mv, ln = sb("stats", [P, T, 6]), sb("mv", [P, T, 2]), sb("ln", [P, 6, T])
        relu, hsq = sb("relu", [P, 2, CH]), sb("hsq", [P, 2, CH])
        h_hi, h_lo = sb("h_hi", [P, HB, CH], F32R), sb("h_lo", [P, HB, CH], F32R)
        y = sb("y", [P, EC, CH])
        mem, part = sb("mem", [P, 2, EC, CH]), sb("part", [P, EC, CH])
        count = sb("count", [P, EC, CH], BF16)
        xres = sb("xres", [P, T, E])
        xsum = sb("xsum", [P, T, E])
        if first:
            xm = sb("xm", [P, T, E])
            mstats, mmv, mln = sb("mstats", [P, T, 6]), sb("mmv", [P, T, 2]), sb("mln", [P, 6, T])
            qk, rq, rest = (sb(n, [P, T, 2 * E]) for n in ("qk", "rq", "rest"))
            prod = sb("prod", [P, 4, E])
            parts = sb("parts", [P, 3, T, 2 * E], BF16)
            qkT = sb("qkT", [P, 3, 4, CH], BF16)
            v = sb("v", [P, T, E])
            cosb, sinb = sb("cosb", [P, TOK // P, 2, D // 2]), sb("sinb", [P, TOK // P, 2, D // 2])
            staged = [rest[:, :, :].rearrange("p t n -> p (t n)"), qk[:, :, :].rearrange("p t n -> p (t n)"),
                      rq[:, 0:3, :].rearrange("p t n -> p (t n)")]
        else:
            ain = sb("ain", [P, T, E])
            xb = sb("xb", [P, T, E])
            x2, xmid = sb("x2", [P, T, E]), sb("xmid", [P, T, E])
            staged = [sb("stage_up", [P, EC * F])[:, :], sb("stage_down", [P, FC * E])[:, :],
                      sb("stage_proj", [P, EC * E])[:, :]]
        split = list(zip(staged, [a[:, :, :].rearrange("p c n -> p (c n)") for a in (up_hi, down_hi, proj_hi)],
                         [a[:, :, :].rearrange("p c n -> p (c n)") for a in (up_lo, down_lo, proj_lo)]))

        tps, yps = pb("tps", [P, EC, CH]), pb("yps", [P, EC, CH])
        ups, gps = pb("ups", [P, 2, CH]), pb("gps", [P, 2, CH])
        gpsb = [gps[:, g, :].bitcast(BF16) for g in range(2)]

        norm_steps = ("stats", "aggr", "var", "std", "rec", "sq", "err", "fix", "rstd", "norm", "T", "hi", "evac")
        names = ["const_in", "w_in", "w_hi", "w_lo", "identb_ok", "x_in", "up_done", "relu_done", "hi_done",
                 "sq_done", "lo_done", "down_done", "y_evac", "spike", "count_T", "sum_done", "sum_out"]
        names += ["pre_" + n for n in norm_steps]
        if first:
            names += ["mid_" + n for n in norm_steps]
            names += ["res_in", "qk_done", "qk_evac", "v_done", "v_evac", "v_out", "rope_mul", "rope_done",
                      "p0_done", "p1_done", "rest_done", "p2_done", "fill_done", "fill_evac", "qkT_out"]
        else:
            names += ["a_in", "a_T", "a_hi", "a_evac", "o_done", "xb_done", "x2_done", "kept", "res_done"]
        s = {n: sem(n) for n in names}
        passed = [sem("passed_pool"), sem("passed_dve")]
        CONSTS = 16 * (4 if first else 2)
        SP = 3 * (STEPS - 1) + 1

        def rows(ap, c):
            return ap[bass.ds(c * CH, CH), :].rearrange("(t p) e -> p t e", p=P)

        def pipeline(eng, body):
            lo, hi, end = (3, NC - 1, NC + 2) if first else (2, NC - 1, NC + 1)

            def at(it, n):
                body(it, n + 1 < NC, n < NC, 1 <= n <= NC, first and n >= 2)

            for n in range(lo):
                at(n, n)
            with eng.Fori(lo, hi) as it:
                at(it, lo)
            for n in range(hi, end):
                at(n, n)

        block = ctx.enter_context(nc.Block())

        @block.sync
        def _(sp):
            sp.dma_start(ident[:, :], w["ident"]).then_inc(s["const_in"], 16)
            sp.dma_start(bias[:, :], w["bv" if first else "bo"].partition_broadcast(P)).then_inc(s["const_in"], 16)
            if first:
                for tab, name in ((cosb, "cos"), (sinb, "sin")):
                    sp.dma_start(tab[:, :, :, :], w[name].rearrange("(t p) (k i) -> p t k i", p=P, k=2))\
                      .then_inc(s["const_in"], 16)
            sp.dma_start(xin[:, :, :], rows(src, 0)).then_inc(s["x_in"], 16)
            if not first:
                sp.dma_start(ain[:, :, :], rows(io["attn"], 0)).then_inc(s["a_in"], 16)
            for st, name in zip(staged, ("up", "down", "qkv" if first else "o")):
                m = w[name]
                sp.dma_start(st.rearrange("p (c n) -> p c n", n=m.shape[1]), m.rearrange("(c p) n -> p c n", p=P))\
                  .then_inc(s["w_in"], 16)

            def body(it, pre, ffn, post, tail):
                if pre:
                    if first:
                        sp.wait_ge(s["pre_norm"], it + 1)
                    else:
                        sp.wait_ge(s["xb_done"], it + 1)
                        sp.wait_ge(s["a_T"], it + 1)
                        sp.dma_start(ain[:, :, :], rows(io["attn"], it + 1)).then_inc(s["a_in"], 16)
                    sp.dma_start(xin[:, :, :], rows(src, it + 1)).then_inc(s["x_in"], 16)
                if post:
                    m = it - 1
                    sp.wait_ge(s["sum_done"], m + 1)
                    sp.dma_start(rows(dst, m), xsum[:, :, :]).then_inc(s["sum_out"], 16)
                if first and ffn:
                    sp.dma_start(xres[:, :, :], rows(src, it)).then_inc(s["res_in"], 16)
                if tail:
                    j = it - 2
                    sp.wait_ge(s["fill_evac"], 6 * j + 6)
                    for a in range(3):
                        sp.dma_start(io["qkT"][a].rearrange("(k p) n -> p k n", p=P)[:, :, bass.ds(j * CH, CH)],
                                     qkT[:, a, :, :]).then_inc(s["qkT_out"], 16)
                if first and post:
                    sp.wait_ge(s["v_evac"], it)
                    sp.dma_start(rows(io["v"], it - 1), v[:, :, :]).then_inc(s["v_out"], 16)

            pipeline(sp, body)
            sp.wait_ge(s["sum_out"], 16 * NC)
            if first:
                sp.wait_ge(s["v_out"], 16 * NC)
                sp.wait_ge(s["qkT_out"], 48 * NC)

        @block.scalar
        def _(act):
            def std(which, c, l):
                act.wait_ge(s[which + "_var"], c + 1)
                act.activation(l[:, 1, :], l[:, 0, :], ACT.Sqrt).then_inc(s[which + "_std"], 1)

            def high(which, c, hi):
                act.wait_ge(s[which + "_T"], c + 1)
                act.activation(hi[:, :, :], tps[:, :, :], ACT.Copy).then_inc(s[which + "_hi"], 1)

            def parts_evac(j, k):
                act.wait_ge(s["fill_done"], 6 * j + k + 1)
                if k == 0:
                    act.wait_ge(s["qkT_out"], 48 * j)
                act.activation(qkT[:, k // 2, 2 * (k % 2):2 * (k % 2) + 2, :],
                               gpsb[k % 2].rearrange("p (k n) -> p k n", k=2), ACT.Copy).then_inc(s["fill_evac"], 1)

            def body(it, pre, ffn, post, tail):
                j = it - 2
                for f in range(FC):
                    if ffn:
                        n = it * FC + f
                        act.wait_ge(s["up_done"], n + 1)
                        if f >= 2 or post:
                            act.wait_ge(s["sq_done"], n - 1)
                        act.activation(relu[:, f % 2, :], ups[:, f % 2, :], ACT.Relu).then_inc(s["relu_done"], 1)
                        act.wait_ge(s["relu_done"], n + 1)
                        if f >= HB or post:
                            act.wait_ge(s["down_done"], n - HB + 1)
                        act.activation(h_hi[:, f % HB, :], relu[:, f % 2, :], ACT.Square).then_inc(s["hi_done"], 1)
                    if first and post and f == 3:
                        std("mid", it - 1, mln)
                    if first and pre and f == 4:
                        std("pre", it + 1, ln)
                    if tail and f == 4:
                        act.wait_ge(s["rope_done"], 2 * T * (j + 1))
                        act.wait_ge(s["fill_done"], 6 * j)
                        act.activation(parts[:, 0, :, :], rq[:, :, :], ACT.Copy).then_inc(s["p0_done"], 1)
                    if tail and f == 5:
                        act.wait_ge(s["rest_done"], j + 1)
                        act.activation(parts[:, 1, :, :], rest[:, :, :], ACT.Copy).then_inc(s["p1_done"], 1)
                    if first and post and f == 6:
                        act.wait_ge(s["qk_done"], T * (it - 1))
                        high("mid", it - 1, mT_hi)
                    if not first and pre and f == 3:
                        act.wait_ge(s["o_done"], it + 1)
                        act.wait_ge(s["a_T"], it + 2)
                        act.activation(mT_hi[:, :, :], tps[:, :, :], ACT.Copy).then_inc(s["a_hi"], 1)
                    if not first and pre and f == 6:
                        std("pre", it + 1, ln)
                if pre:
                    act.wait_ge(s["up_done"], FC * it + FC)
                    high("pre", it + 1, xT_hi)
                if tail:
                    parts_evac(j, 0)
                if ffn:
                    act.wait_ge(s["down_done"], FC * it + FC)
                    act.wait_ge(s["spike"], SP * it)
                    act.activation(y[:, :, :], yps[:, :, :], ACT.Copy).then_inc(s["y_evac"], 1)
                if tail:
                    for k in range(1, 6):
                        parts_evac(j, k)
                if first and post:
                    for t in range(T):
                        act.wait_ge(s["qk_done"], T * (it - 1) + t + 1)
                        if t == 0:
                            act.wait_ge(s["rope_done"], 2 * T * (it - 1))
                        act.activation(qk[:, t, :], gps[:, t % 2, :], ACT.Copy).then_inc(s["qk_evac"], 1)

            act.wait_ge(s["w_in"], 48)
            for st, hi, _ in split:
                act.activation(hi, st, ACT.Copy).then_inc(s["w_hi"], 1)
            act.wait_ge(s["const_in"], CONSTS)
            act.activation(identb[:, :], ident[:, :], ACT.Copy).then_inc(s["identb_ok"], 1)
            if not first:
                act.wait_ge(s["a_T"], 1)
                act.activation(mT_hi[:, :, :], tps[:, :, :], ACT.Copy).then_inc(s["a_hi"], 1)
            std("pre", 0, ln)
            high("pre", 0, xT_hi)
            pipeline(act, body)

        @block.vector
        def _(dve):
            def norm_stats(which, c, x, st, m, l):
                for t in range(T):
                    dve.bn_stats(st[:, t, :], x[:, t, :]).then_inc(s[which + "_stats"], 1)
                dve.wait_ge(s[which + "_stats"], T * c + T)
                dve.sem_inc(passed[1], 1)
                for t in range(T):
                    dve.bn_aggr(m[:, t, :], st[:, t, :]).then_inc(s[which + "_aggr"], 1)
                dve.wait_ge(s[which + "_aggr"], T * c + T)
                dve.tensor_scalar(l[:, 0, :], m[:, :, 1], EPS, None, ALU.add).then_inc(s[which + "_var"], 1)

            def norm(which, c, x, o, m, l):
                dve.wait_ge(s[which + "_std"], c + 1)
                dve.reciprocal(l[:, 2, :], l[:, 1, :]).then_inc(s[which + "_rec"], 1)
                dve.wait_ge(s[which + "_rec"], c + 1)
                dve.tensor_tensor(l[:, 3, :], l[:, 2, :], l[:, 2, :], ALU.mult).then_inc(s[which + "_sq"], 1)
                dve.wait_ge(s[which + "_sq"], c + 1)
                dve.tensor_tensor(l[:, 4, :], l[:, 3, :], l[:, 0, :], ALU.mult).then_inc(s[which + "_err"], 1)
                dve.wait_ge(s[which + "_err"], c + 1)
                dve.tensor_scalar(l[:, 5, :], l[:, 4, :], -0.5, 1.5, ALU.mult, ALU.add).then_inc(s[which + "_fix"], 1)
                dve.wait_ge(s[which + "_fix"], c + 1)
                dve.tensor_tensor(l[:, 3, :], l[:, 2, :], l[:, 5, :], ALU.mult).then_inc(s[which + "_rstd"], 1)
                dve.wait_ge(s[which + "_rstd"], c + 1)
                dve.wait_ge(s[which + "_T"], c)
                for t in range(T):
                    last = dve.tensor_scalar(o[:, t, :], x[:, t, :], m[:, t, 0:1], l[:, 3, t:t + 1],
                                             ALU.subtract, ALU.mult)
                last.then_inc(s[which + "_norm"], 1)

            def low(which, c, hi, lo):
                dve.wait_ge(s[which + "_hi"], c + 1)
                dve.tensor_tensor(lo[:, :, :], tps[:, :, :], hi[:, :, :].bitcast(F32), ALU.subtract)\
                   .then_inc(s[which + "_evac"], 1)

            def spikes(c, k0, k1):
                for k in range(k0, k1):
                    step, what = (k - 1) // 3, (k - 1) % 3
                    cur, sign, above = (y, 1.0, ALU.is_gt) if step == 0 else (mem[:, (step - 1) % 2], -1.0, ALU.is_lt)
                    cur = cur[:, :, :] if step == 0 else cur
                    if k == 0:
                        dve.wait_ge(s["y_evac"], c + 1)
                        dve.wait_ge(s["count_T"], c)
                        dve.tensor_scalar(count[:, :, :], y[:, :, :], THRESHOLD, None, ALU.is_gt)\
                           .then_inc(s["spike"], 1)
                        continue
                    dve.wait_ge(s["spike"], SP * c + k)
                    if what == 0:
                        dve.scalar_tensor_tensor(out=part[:, :, :], in0=cur, scalar=sign * BETA, in1=y[:, :, :],
                                                 op0=ALU.mult, op1=ALU.add).then_inc(s["spike"], 1)
                    elif what == 1:
                        dve.scalar_tensor_tensor(out=mem[:, step % 2], in0=cur, scalar=sign * THRESHOLD,
                                                 in1=part[:, :, :], op0=above, op1=ALU.subtract)\
                           .then_inc(s["spike"], 1)
                    else:
                        dve.scalar_tensor_tensor(out=count[:, :, :], in0=mem[:, step % 2], scalar=-THRESHOLD,
                                                 in1=count[:, :, :], op0=ALU.is_lt, op1=ALU.add)\
                           .then_inc(s["spike"], 1)

            def sum_(c):
                dve.wait_ge(s["count_T"], c + 1)
                if first:
                    dve.wait_ge(s["res_in"], 16 * (c + 1))
                else:
                    dve.wait_ge(s["res_done"], c + 1)
                dve.wait_ge(s["sum_out"], 16 * c)
                dve.scalar_tensor_tensor(out=xsum[:, :, :].rearrange("p t e -> p (t e)"), in0=gpsb[0],
                                         scalar=0.5 / STEPS, in1=xres[:, :, :].rearrange("p t e -> p (t e)"),
                                         op0=ALU.mult, op1=ALU.add).then_inc(s["sum_done"], 1)

            def attn_sum(c):
                dve.wait_ge(s["o_done"], c + 1)
                dve.wait_ge(s["xb_done"], c + 1)
                dve.wait_ge(s["kept"], c)
                dve.tensor_tensor(x2[:, :, :].rearrange("p t e -> p (t e)"), gps[:, :, :].rearrange("p g n -> p (g n)"),
                                  xb[:, :, :].rearrange("p t e -> p (t e)"), ALU.add).then_inc(s["x2_done"], 1)
                dve.wait_ge(s["x2_done"], c + 1)

            def body(it, pre, ffn, post, tail):
                j = it - 2
                for f in range(FC):
                    if ffn:
                        n = it * FC + f
                        dve.wait_ge(s["sq_done"], n + 1)
                        dve.wait_ge(s["hi_done"], n + 1)
                        if f >= HB or post:
                            dve.wait_ge(s["down_done"], n - HB + 1)
                        dve.tensor_tensor(h_lo[:, f % HB, :], hsq[:, f % 2, :], h_hi[:, f % HB, :].bitcast(F32),
                                          ALU.subtract).then_inc(s["lo_done"], 1)
                    if first:
                        if post and f == 2:
                            sum_(it - 1)
                            dve.wait_ge(s["sum_done"], it)
                            norm_stats("mid", it - 1, xsum, mstats, mmv, mln)
                        if post and f == 3:
                            norm("mid", it - 1, xsum, xm, mmv, mln)
                        if pre and f == 4:
                            dve.wait_ge(s["x_in"], 16 * (it + 2))
                            norm_stats("pre", it + 1, xin, stats, mv, ln)
                        if pre and f == 5:
                            norm("pre", it + 1, xin, xn, mv, ln)
                        if tail and f == 4:
                            dve.wait_ge(s["p0_done"], j + 1)
                            dve.tensor_tensor(rest[:, :, :], rq[:, :, :], parts[:, 0, :, :], ALU.subtract)\
                               .then_inc(s["rest_done"], 1)
                        if tail and f == 5:
                            dve.wait_ge(s["p1_done"], j + 1)
                            dve.tensor_tensor(parts[:, 2, :, :], rest[:, :, :], parts[:, 1, :, :], ALU.subtract)\
                               .then_inc(s["p2_done"], 1)
                        if post and f == 6:
                            low("mid", it - 1, mT_hi, mT_lo)
                    else:
                        if post and f < 5:
                            spikes(it - 1, 3 * f, min(3 * f + 3, SP))
                        if pre and f == 3:
                            low("a", it + 1, mT_hi, mT_lo)
                        if pre and f == 5:
                            attn_sum(it + 1)
                            norm_stats("pre", it + 1, x2, stats, mv, ln)
                        if pre and f == 6:
                            norm("pre", it + 1, x2, xn, mv, ln)
                        if post and f == 7:
                            sum_(it - 1)
                if pre:
                    low("pre", it + 1, xT_hi, xT_lo)
                if first and ffn:
                    spikes(it, 0, SP)
                if first and post:
                    dve.wait_ge(s["v_done"], it)
                    dve.wait_ge(s["v_out"], 16 * (it - 1))
                    dve.tensor_tensor(v[:, :, :], tps[:, :, :].rearrange("p c (t e) -> p (c t) e", e=E),
                                      bias[:, :].unsqueeze(1).broadcast_to([P, T, E]), ALU.add)\
                       .then_inc(s["v_evac"], 1)

            for i, (st, hi, lo) in enumerate(split):
                dve.wait_ge(s["w_hi"], i + 1)
                dve.tensor_tensor(lo, st, hi.bitcast(F32), ALU.subtract).then_inc(s["w_lo"], 1)
            if first:
                dve.wait_ge(s["x_in"], 16)
                norm_stats("pre", 0, xin, stats, mv, ln)
                norm("pre", 0, xin, xn, mv, ln)
            else:
                low("a", 0, mT_hi, mT_lo)
                attn_sum(0)
                norm_stats("pre", 0, x2, stats, mv, ln)
                norm("pre", 0, x2, xn, mv, ln)
            low("pre", 0, xT_hi, xT_lo)
            pipeline(dve, body)

        @block.gpsimd
        def _(pool):
            def rope(j, t):
                pool.wait_ge(s["qk_evac"], T * j + t + 1)
                x = qk[:, t, :].rearrange("p (k h i two) -> p k h i two", k=2, h=H, two=2)
                o = rq[:, t, :].rearrange("p (h i two) -> p h i two", i=D // 2, two=2)

                def table(tab):
                    return tab[:, bass.ds(T * j + t, 1), :, :].rearrange("p o k i -> p (o k) i").unsqueeze(2)\
                        .broadcast_to([P, 2, H, D // 2])

                for n, (half, tab) in enumerate(((0, cosb), (1, sinb), (0, sinb), (1, cosb))):
                    pool.tensor_tensor(prod[:, n, :].rearrange("p (k h i) -> p k h i", k=2, h=H), x[:, :, :, :, half],
                                       table(tab), ALU.mult).then_inc(s["rope_mul"], 1)
                pool.wait_ge(s["rope_mul"], 4 * (T * j + t + 1))
                if t == 0:
                    pool.wait_ge(s["rest_done"], j)
                p4 = prod[:, :, :].rearrange("p n (h i) -> p n h i", i=D // 2)
                pool.tensor_tensor(o[:, :, :, 0], p4[:, 0], p4[:, 1], ALU.subtract).then_inc(s["rope_done"], 1)
                pool.tensor_tensor(o[:, :, :, 1], p4[:, 2], p4[:, 3], ALU.add).then_inc(s["rope_done"], 1)
                pool.wait_ge(s["rope_done"], 2 * (T * j + t + 1))

            def add_bias(c):
                pool.wait_ge(s["x_in"], 16 * (c + 1))
                pool.wait_ge(s["x2_done"], c)
                pool.tensor_tensor(xb[:, :, :], xin[:, :, :], bias[:, :].unsqueeze(1).broadcast_to([P, T, E]), ALU.add)\
                    .then_inc(s["xb_done"], 1)

            def keep(it, ffn, post):
                if post:
                    pool.wait_ge(s["kept"], it)
                    pool.wait_ge(s["sum_done"], it - 1)
                    pool.sem_inc(passed[0], 1)
                    pool.tensor_copy(xres[:, :, :], xmid[:, :, :]).then_inc(s["res_done"], 1)
                    pool.wait_ge(s["res_done"], it)
                if ffn:
                    pool.wait_ge(s["x2_done"], it + 1)
                    pool.sem_inc(passed[0], 1)
                    pool.tensor_copy(xmid[:, :, :], x2[:, :, :]).then_inc(s["kept"], 1)

            def body(it, pre, ffn, post, tail):
                for f in range(FC):
                    if ffn:
                        n = it * FC + f
                        pool.wait_ge(s["relu_done"], n + 1)
                        if f >= 2 or post:
                            pool.wait_ge(s["lo_done"], n - 1)
                        pool.tensor_tensor(hsq[:, f % 2, :], relu[:, f % 2, :], relu[:, f % 2, :], ALU.mult)\
                            .then_inc(s["sq_done"], 1)
                    if tail and f < T:
                        rope(it - 2, f)
                    if not first and f == 0:
                        keep(it, ffn, post)
                    if not first and pre and f == 1:
                        add_bias(it + 1)

            pool.wait_ge(s["const_in"], CONSTS)
            if first:
                pool.wait_ge(s["w_lo"], 3)
            else:
                add_bias(0)
            pipeline(pool, body)

        @block.tensor
        def _(pe):
            def up(it, f, post):
                n = it * FC + f
                if f == 0:
                    pe.wait_ge(s["pre_evac"], it + 1)
                if f >= 2 or post:
                    pe.wait_ge(s["relu_done"], n - 1)
                for i, (wt, x, c) in enumerate([(a, b, c) for c in range(EC) for a, b in
                                                ((up_hi, xT_hi), (up_hi, xT_lo), (up_lo, xT_hi))]):
                    last = pe.matmul(ups[:, f % 2, :], wt[:, c, f * P:(f + 1) * P], x[:, c, :],
                                     start=(i == 0), stop=(i == 3 * EC - 1))
                last.then_inc(s["up_done"], 1)

            def down(it, f):
                if f == 0:
                    pe.wait_ge(s["y_evac"], it)
                pe.wait_ge(s["lo_done"], it * FC + f + 1)
                for c in range(EC):
                    for i, (wt, h) in enumerate(((down_hi, h_hi), (down_hi, h_lo), (down_lo, h_hi))):
                        last = pe.matmul(yps[:, c, :], wt[:, f, c * P:(c + 1) * P], h[:, f % HB, :],
                                         start=(f == 0 and i == 0), stop=(f == FC - 1 and i == 2))
                last.then_inc(s["down_done"], 1)

            def turn(x, done):
                for t in range(T):
                    for c in range(EC):
                        last = pe.transpose(tps[:, c, t * P:(t + 1) * P], x[:, t, c * P:(c + 1) * P], ident[:, :])
                last.then_inc(s[done], 1)

            def count_turn(c, pre):
                pe.wait_ge(s["spike"], SP * (c + 1))
                pe.wait_ge(s["sum_done"], c)
                if first:
                    pe.wait_ge(s["qk_evac"], T * c)
                elif pre:
                    pe.wait_ge(s["x2_done"], c + 3)
                for t in range(T):
                    for k in range(EC):
                        last = pe.transpose(gpsb[0][:, t * E + k * P:t * E + (k + 1) * P],
                                            count[:, k, t * P:(t + 1) * P], identb[:, :])
                last.then_inc(s["count_T"], 1)

            def fill(j, k, post=False):
                if k == 0:
                    pe.wait_ge(s["p2_done"], j + 1)
                    if post:
                        pe.wait_ge(s["sum_done"], j + 2)
                if k >= 2:
                    pe.wait_ge(s["fill_evac"], 6 * j + k - 1)
                for b in range(2):
                    blk = 2 * (k % 2) + b
                    for t in range(T):
                        last = pe.transpose(gpsb[k % 2][:, b * CH + t * P:b * CH + (t + 1) * P],
                                            parts[:, k // 2, t, blk * P:(blk + 1) * P], identb[:, :])
                last.then_inc(s["fill_done"], 1)

            def project(out, t, c0, c1):
                for i, (wt, x, c) in enumerate([(a, b, c) for c in range(EC) for a, b in
                                                ((proj_hi, mT_hi), (proj_hi, mT_lo), (proj_lo, mT_hi))]):
                    last = pe.matmul(out, x[:, c, t * P:(t + 1) * P], wt[:, c, c0:c1],
                                     start=(i == 0), stop=(i == 3 * EC - 1))
                return last

            def attn_turn(c):
                pe.wait_ge(s["a_in"], 16 * (c + 1))
                pe.wait_ge(s["pre_evac"], c)
                turn(ain, "a_T")

            def attn_out(c, post):
                pe.wait_ge(s["a_evac"], c + 1)
                if post:
                    pe.wait_ge(s["sum_done"], c - 2)
                for t in range(T):
                    last = project(gps[:, t // 2, (t % 2) * E:(t % 2 + 1) * E], t, 0, E)
                last.then_inc(s["o_done"], 1)

            def body(it, pre, ffn, post, tail):
                j, m = it - 2, it - 1
                for f in range(FC):
                    if ffn:
                        up(it, f, post)
                    if first and post and f == 2:
                        count_turn(m, pre)
                    if first and post and f == 5:
                        pe.wait_ge(s["mid_norm"], it)
                        pe.wait_ge(s["v_evac"], m)
                        if ffn:
                            pe.wait_ge(s["pre_evac"], it + 1)
                        turn(xm, "mid_T")
                    if not first and pre and f == 2:
                        attn_turn(it + 1)
                    if not first and pre and f == 4:
                        attn_out(it + 1, post)
                    if not first and post and f == 6:
                        count_turn(m, pre)
                    if ffn and f >= LAG:
                        down(it, f - LAG)
                if pre:
                    pe.wait_ge(s["pre_norm"], it + 2)
                    if first:
                        pe.wait_ge(s["mid_evac"], it)
                    else:
                        pe.wait_ge(s["a_evac"], it + 2)
                    turn(xn, "pre_T")
                if ffn:
                    down(it, FC - 2)
                if tail:
                    fill(j, 0, post)
                if ffn:
                    down(it, FC - 1)
                if tail:
                    fill(j, 1)
                if first and post:
                    pe.wait_ge(s["mid_evac"], it)
                    if pre:
                        pe.wait_ge(s["pre_evac"], it + 2)
                    for t in range(T):
                        last = project(tps[:, t // 2, (t % 2) * E:(t % 2 + 1) * E], t, 2 * E, 3 * E)
                        if tail and t % 2 == 1:
                            fill(j, 2 + t // 2)
                    last.then_inc(s["v_done"], 1)
                    if tail:
                        fill(j, 4)
                        fill(j, 5)
                    for t in range(T):
                        if t < 2:
                            if tail:
                                pe.wait_ge(s["fill_evac"], 6 * j + 5 + t)
                        else:
                            pe.wait_ge(s["qk_evac"], T * m + t - 1)
                        if t == 0:
                            pe.wait_ge(s["sum_done"], it)
                        project(gps[:, t % 2, :], t, 0, 2 * E).then_inc(s["qk_done"], 1)
                elif tail:
                    for k in range(2, 6):
                        fill(j, k)

            pe.wait_ge(s["const_in"], CONSTS)
            pe.wait_ge(s["identb_ok"], 1)
            pe.wait_ge(s["w_lo"], 3)
            if not first:
                attn_turn(0)
                attn_out(0, False)
            pe.wait_ge(s["pre_norm"], 1)
            turn(xn, "pre_T")
            pipeline(pe, body)


def attention_phase(nc, w, io):
    with ExitStack() as ctx:
        def sb(name, shape, dt=F32):
            return ctx.enter_context(nc.sbuf_tensor(name, shape, dt))

        def pb(name, shape, dt=F32):
            return ctx.enter_context(nc.psum_tensor(name, shape, dt))

        def sem(name):
            return ctx.enter_context(nc.semaphore(name))

        KB = S // P
        NJ = S // CH
        PAIRS = B * NG // 2
        PBUF = 4
        VW = 32

        qT = [sb(f"qT{p}", [P, NJ, G, CH], BF16) for p in range(2)]
        kT = [sb(f"kT{p}", [P, G, S], BF16) for p in range(2)]
        v_in = [sb(f"v_in{p}", [P, KB, G * D]) for p in range(2)]
        v_w = [sb(f"v_w{p}", [P, KB, G, VW]) for p in range(2)]
        probs = sb("probs", [P, PBUF, G, CH])
        ident, identb = sb("ident_b", [P, P]), sb("identb_b", [P, P], BF16)
        mask, maskb = sb("mask_b", [P, P]), sb("maskb", [P, P], BF16)
        maxes = sb("maxes", [P, 2, G, T, NJ])
        negmax, negrest = sb("negmax", [P, G * T]), sb("negrest", [P, G * T])
        negparts = sb("negparts", [P, P // (G * T), G * T], BF16)
        shiftT = sb("shiftT", [3 * G * T, P], BF16)
        osum = sb("osum", [P, CH])
        denom = sb("denom", [P, T * G])
        att = sb("att", [P, T, G * D])

        s_ps = [pb(f"s_ps{p}", [P, 2, CH]) for p in range(2)]
        m_ps = pb("m_ps", [P, 2, CH])
        o_ps = pb("o_ps", [P, CH])
        t_ps = pb("t_ps", [P, CH])

        const_in, const_ok, ones_ok = sem("const_in_b"), sem("const_ok_b"), sem("ones_ok")
        qk_in = [sem(f"qk_in{p}") for p in range(2)]
        vs_in = [sem(f"vs_in{p}") for p in range(2)]
        v_ready, s_done, exp_done, diag_done, pv_done = (sem(n) for n in (
            "v_ready", "s_done", "exp_done", "diag_done", "pv_done"))
        max_done, max_read, neg_done, neg_step, neg_turned, neg_out, shift_in = (sem(n) for n in (
            "max_done", "max_read", "neg_done", "neg_step", "neg_turned", "neg_out", "shift_in"))
        neg_zero = sem("neg_zero")
        passed = sem("passed_b")
        o_read, o_turned, denom_done, att_done, att_out = (sem(n) for n in (
            "o_read", "o_turned", "denom_done", "att_done", "att_out"))

        def step_no(n, j):
            return NJ * n + j

        def exp_units(n, j, i):
            return 80 * n + 4 * j * (j + 1) + 2 * i

        def key_blocks(n, j, i):
            return 40 * n + 2 * j * (j + 1) + i

        SLOTS = NJ * (NJ + 1) * T // 2
        UNITS = [(j, t, h, k, CH if k < j else P * (t + 1))
                 for j in range(NJ) for t in range(T) for h in range(G) for k in range(j + 1)]
        MAX_FROM, MAX_TO = -20, 20

        def place_units():
            cost = [u[4] + 110 for u in UNITS]
            room = []
            for s in range(MAX_FROM, MAX_TO):
                j, b = [(j, b) for j in range(NJ) for b in range(T * j + T)][s % SLOTS]
                room.append(1 + T - max(0, b - T * j))
            slots, done, full, u = {}, 0, 0, 0
            for s, r in zip(range(MAX_FROM, MAX_TO), room):
                full += r * sum(cost) / sum(room)
                slots[s] = []
                while u < len(UNITS) and (done + cost[u] / 2 <= full):
                    slots[s].append(u)
                    done += cost[u]
                    u += 1
            assert u == len(UNITS)
            return slots

        unit_slots = place_units()
        NEG_OPS = 5

        def vector_items():
            items, pending = {}, []
            for s in sorted(unit_slots):
                items[s] = []
                for u in unit_slots[s]:
                    items[s].append(("unit", u))
                    if u + 1 == len(UNITS) or UNITS[u + 1][0] > UNITS[u][0]:
                        pending = [(UNITS[u][0], k) for k in range(NEG_OPS)]
                    if pending:
                        items[s].append(("negate", pending.pop(0)))
            items[s] += [("negate", x) for x in pending]
            return items

        vector_slots = vector_items()
        found = [max(s for s in vector_slots if ("negate", (m, NEG_OPS - 1)) in vector_slots[s]) for m in range(NJ)]
        SUM = 3
        sum_slots = [2 * j * (j + 1) + SUM for j in range(NJ)]
        turn_slots = {f + 1: m for m, f in enumerate(found)}
        out_slots = {x if x % SLOTS in sum_slots else x + 1: m for x, m in turn_slots.items()}

        def due(slots, s):
            return [(ahead, slots[x]) for ahead, x in ((0, s), (1, s - SLOTS)) if x in slots]

        def turns_before_sum(j):
            return sum(x <= sum_slots[j] for x in turn_slots) + sum(SLOTS + x <= sum_slots[j] for x in turn_slots)

        def sums_before_turn(m):
            x = found[m] + 1
            return sum(y < x for y in sum_slots) - sum(y >= x + SLOTS for y in sum_slots) - 1

        LOADS = 16 * NT * (NJ + 1)
        FREE_P, FREE_S, FREE_M = PBUF, 2, 2

        def wait(eng, sem, value):
            if not isinstance(value, int) or value > 0:
                eng.wait_ge(sem, value)

        def preceding(dn, j):
            return (dn, j - 1) if j else (dn - 1, NJ - 1)

        def exists(i, dn):
            return not isinstance(i, int) or 2 * i + dn < B * NG

        def steps(eng, body):
            turn = [(dn, j) for dn in range(2) for j in range(NJ)][2:] + [(2, 0), (2, 1)]
            body(0, 0, 0, False)
            body(0, 0, 1, False)
            with eng.Fori(0, PAIRS - 1) as i:
                for dn, j in turn:
                    body(i, dn, j, False)
            for dn, j in turn[:-2]:
                body(PAIRS - 1, dn, j, (dn, j) == (1, NJ - 1))

        def place(i, dn):
            i, dn = i + dn // 2, dn % 2
            return (i // 2) * S, ((i % 2) * 2 + dn) * (G * D)

        block = ctx.enter_context(nc.Block())

        @block.sync
        def _(sp):
            sp.dma_start(ident[:, :], w["ident"]).then_inc(const_in, 16)
            sp.dma_start(mask[:, :], w["mask"]).then_inc(const_in, 16)

            def load(i, dn, terms):
                tok, row = place(i, dn)
                p = dn % 2
                for m in terms:
                    q, k = (io["qkT"][a, bass.ds(row + first, G * D), bass.ds(tok, S)] for a, first in
                            ((QS[m], 0), (KS[m], E)))
                    for j in range(NJ):
                        sp.dma_start(qT[p][D * m:D * (m + 1), j, :, :],
                                     q[:, j * CH:(j + 1) * CH].rearrange("(h d) t -> d h t", d=D))\
                          .then_inc(qk_in[p], 16)
                    sp.dma_start(kT[p][D * m:D * (m + 1), :, :], k.rearrange("(h d) t -> d h t", d=D))\
                      .then_inc(qk_in[p], 16)
                    if m == 0:
                        sp.dma_start(v_in[p][:, :, :], io["v"][bass.ds(tok, S), bass.ds(row, G * D)]
                                     .rearrange("(k p) n -> p k n", p=P)).then_inc(vs_in[p], 16)

            def shift(i, dn, j):
                n = 2 * i + dn
                sp.wait_ge(neg_out, step_no(n, j) + 1)
                for a in range(3):
                    sp.dma_start(qT[dn % 2][KR + a:KR + a + 1, j, :, :],
                                 shiftT[a * G * T:(a + 1) * G * T, :]).then_inc(shift_in, 16)

            def body(i, dn, j, final):
                n = 2 * i + dn
                if j < 3 and exists(i, dn + 1):
                    if j == 0 and (dn > 0):
                        sp.wait_ge(s_done, exp_units(n, 0, 0))
                        sp.wait_ge(v_ready, n)
                    load(i, dn + 1, (2 * j, 2 * j + 1))
                for b in range(T * j + T):
                    if b == SUM and (dn, j) != (0, 0):
                        store(i, *preceding(dn, j))
                    for ahead, m in due(out_slots, key_blocks(0, j, b)):
                        if exists(i, dn + ahead):
                            shift(i, dn + ahead, m)
                if final:
                    store(i, dn, j)

            def store(i, dn, j):
                tok, row = place(i, dn)
                sp.wait_ge(att_done, step_no(2 * i + dn, j) + 1)
                sp.dma_start(io["attn"][bass.ds(tok + j * CH, CH), bass.ds(row, G * D)]
                             .rearrange("(t p) n -> p t n", p=P), att[:, :, :]).then_inc(att_out, 16)

            load(0, 0, range(NT))
            for x in range(MAX_FROM, 0):
                if x in out_slots:
                    shift(0, 0, out_slots[x])
            steps(sp, body)
            sp.wait_ge(att_out, 16 * NJ * B * NG)

        @block.gpsimd
        def _(pool):
            for p in range(2):
                pool.memset(kT[p][KR:KC, :, :], 1.0).then_inc(ones_ok, 1)
                pool.wait_ge(ones_ok, 3 * p + 1)
                pool.memset(v_w[p][:, :, :, :], 0.0).then_inc(ones_ok, 1)
                pool.wait_ge(ones_ok, 3 * p + 2)
                pool.memset(v_w[p][:, :, :, D:D + 1], 1.0).then_inc(ones_ok, 1)
                pool.wait_ge(ones_ok, 3 * p + 3)

            def body(i, dn, j, final):
                n = 2 * i + dn
                for a in range(T):
                    pool.wait_ge(exp_done, FREE_S + exp_units(n, j, T * j + a + 1))
                    tile = probs[:, (T * j + a) % PBUF, :, P * a:P * (a + 1)]
                    pool.sem_inc(passed, 1)
                    pool.affine_select(out=tile, in_=tile, compare_op=ALU.is_ge, fill=0.0, base=0,
                                       pattern=[[0, G], [1, P]], channel_multiplier=-1).then_inc(diag_done, 1)

            steps(pool, body)

        @block.scalar
        def _(act):
            act.sem_inc(exp_done, FREE_S)
            act.wait_ge(const_in, 32)
            act.activation(identb[:, :], ident[:, :], ACT.Copy).then_inc(const_ok, 1)
            act.activation(maskb[:, :], mask[:, :], ACT.Copy).then_inc(const_ok, 1)

            def widen(i, dn):
                act.wait_ge(vs_in[dn % 2], 16 * (i + dn // 2 + 1))
                act.activation(v_w[dn % 2][:, :, :, 0:D].rearrange("p k h d -> p (k h) d"),
                               v_in[dn % 2][:, :, :].rearrange("p k (h d) -> p (k h) d", d=D), ACT.Copy)\
                    .then_inc(v_ready, 1)

            def read_sum(i, dn, j):
                n = 2 * i + dn
                act.wait_ge(pv_done, FREE_P + key_blocks(n, j, T * j + T))
                act.wait_ge(o_turned, step_no(n, j))
                act.activation(osum[:, :], o_ps[:, :], ACT.Copy).then_inc(o_read, 1)

            def body(i, dn, j, final):
                n = 2 * i + dn
                for b in range(T * j + T):
                    off = max(0, b - T * j) * P
                    act.wait_ge(pv_done, key_blocks(n, j, b) + 1)
                    for hp in range(2):
                        act.wait_ge(s_done, exp_units(n, j, b) + hp + 1)
                        act.activation(probs[:, b % PBUF, 2 * hp:2 * hp + 2, off:CH], s_ps[hp][:, :, off:CH], ACT.Exp)\
                           .then_inc(exp_done, 1)
                    if b == 1 and (dn, j) != (0, 0):
                        read_sum(i, *preceding(dn, j))
                if j == 1 and exists(i, dn + 1):
                    widen(i, dn + 1)
                if final:
                    read_sum(i, dn, j)

            act.wait_ge(ones_ok, 6)
            widen(0, 0)
            steps(act, body)

        @block.vector
        def _(dve):
            dve.sem_inc(max_read, FREE_M)
            dve.memset(negparts[:, :, :], 0.0).then_inc(neg_zero, 1)
            dve.wait_ge(neg_zero, 1)

            def unit(i, dn, u):
                n = 2 * i + dn
                j, t, h, k, width = UNITS[u]
                dve.wait_ge(max_done, len(UNITS) * n + u + 1)
                dve.tensor_reduce(maxes[:, j % 2, h, t, k:k + 1], m_ps[:, u % 2, 0:width], AX.X, ALU.max)\
                   .then_inc(max_read, 1)

            def negate(i, dn, j, k):
                n = 2 * i + dn
                t = step_no(n, j)
                if k == 0:
                    dve.wait_ge(max_read, FREE_M + len(UNITS) * n + 8 * (j + 1) * (j + 2))
                    dve.tensor_reduce(negmax[:, :], maxes[:, j % 2, :, :, 0:j + 1].rearrange("p h t k -> p (h t) k"), AX.X,
                                      ALU.max, negate=True).then_inc(neg_step, 1)
                elif k == 1:
                    dve.wait_ge(neg_step, 4 * t + 1)
                    wait(dve, neg_turned, t)
                    dve.tensor_copy(negparts[:, 0, :], negmax[:, :]).then_inc(neg_step, 1)
                elif k == 2:
                    dve.wait_ge(neg_step, 4 * t + 2)
                    dve.tensor_tensor(negrest[:, :], negmax[:, :], negparts[:, 0, :], ALU.subtract).then_inc(neg_step, 1)
                elif k == 3:
                    dve.wait_ge(neg_step, 4 * t + 3)
                    dve.tensor_copy(negparts[:, 1, :], negrest[:, :]).then_inc(neg_step, 1)
                else:
                    dve.wait_ge(neg_step, 4 * t + 4)
                    dve.tensor_tensor(negparts[:, 2, :], negrest[:, :], negparts[:, 1, :], ALU.subtract)\
                       .then_inc(neg_done, 1)

            def send(i, dn, j):
                t = step_no(2 * i + dn, j)
                dve.wait_ge(neg_turned, t + 1)
                wait(dve, shift_in, 48 * t)
                dve.tensor_copy(shiftT[:, :], t_ps[:, 0:P // 2].bitcast(BF16)[0:3 * G * T, :]).then_inc(neg_out, 1)

            def normalise(i, dn, j):
                n = 2 * i + dn
                t = step_no(n, j)
                dve.wait_ge(o_turned, t + 1)
                sums = t_ps[:, :].rearrange("p (g w) -> p g w", w=VW)
                dve.reciprocal(denom[:, :].unsqueeze(2), sums[:, :, D:D + 1]).then_inc(denom_done, 1)
                dve.wait_ge(denom_done, t + 1)
                dve.wait_ge(att_out, 16 * t)
                dve.tensor_tensor(att[:, :, :].rearrange("p t (h d) -> p (t h) d", d=D), sums[:, :, 0:D],
                                  denom[:, :].unsqueeze(2).broadcast_to([P, T * G, D]), ALU.mult)\
                   .then_inc(att_done, 1)

            def slot(i, dn, x, ahead):
                for kind, what in vector_slots.get(x, []):
                    if kind == "unit":
                        unit(i, dn + ahead, what)
                    else:
                        negate(i, dn + ahead, *what)
                if x in out_slots:
                    send(i, dn + ahead, out_slots[x])

            def body(i, dn, j, final):
                for b in range(T * j + T):
                    x = key_blocks(0, j, b)
                    slot(i, dn, x, 0)
                    if exists(i, dn + 1):
                        slot(i, dn, x - SLOTS, 1)
                    if b == SUM and (dn, j) != (0, 0):
                        normalise(i, *preceding(dn, j))
                if final:
                    normalise(i, dn, j)

            for x in range(MAX_FROM, 0):
                slot(0, 0, x, 0)
            steps(dve, body)

        @block.tensor
        def _(pe):
            pe.sem_inc(pv_done, FREE_P)

            def find(i, dn, u):
                n = 2 * i + dn
                j, t, h, k, width = UNITS[u]
                if u == 0:
                    pe.wait_ge(qk_in[dn % 2], LOADS * (i + dn // 2 + 1))
                pe.wait_ge(max_read, len(UNITS) * n + u + 1)
                q = qT[dn % 2][0:KR, j, h, t * P:(t + 1) * P]
                mm = pe.matmul(m_ps[:, u % 2, 0:width], q, kT[dn % 2][0:KR, h, k * CH:k * CH + width],
                               start=True, stop=(k < j))
                if k == j:
                    mm = pe.matmul(m_ps[:, u % 2, width - P:width], identb[:, :], maskb[:, :], start=False, stop=True)
                mm.then_inc(max_done, 1)

            def turn_max(i, dn, j):
                n = 2 * i + dn
                wait(pe, att_done, NJ * n + sums_before_turn(j))
                wait(pe, neg_out, step_no(n, j))
                pe.wait_ge(neg_done, step_no(n, j) + 1)
                pe.transpose(t_ps[:, 0:P // 2].bitcast(BF16), negparts[:, :, :].rearrange("p a c -> p (a c)"),
                             identb[:, :]).then_inc(neg_turned, 1)

            def turn_sum(i, dn, j, final=False):
                n = 2 * i + dn
                wait(pe, att_done, step_no(n, j))
                turned = NJ * (n + (j + 1) // NJ) + turns_before_sum((j + 1) % NJ)
                if exists(i, dn + 1):
                    pe.wait_ge(neg_out, turned)
                else:
                    pe.wait_ge(neg_out, min(turned, NJ * B * NG))
                pe.wait_ge(o_read, step_no(n, j) + 1)
                for t in range(T):
                    mm = pe.transpose(t_ps[:, t * P:(t + 1) * P], osum[:, t * P:(t + 1) * P], ident[:, :])
                mm.then_inc(o_turned, 1)

            def scores(i, dn, j, b, hp):
                n = 2 * i + dn
                off = max(0, b - T * j) * P
                if b == 0 and hp == 0:
                    pe.wait_ge(shift_in, 48 * (step_no(n, j) + 1))
                pe.wait_ge(exp_done, exp_units(n, j, b) + hp + 1)
                for h in range(2):
                    mm = pe.matmul(s_ps[hp][:, h, off:CH], kT[dn % 2][0:KC, 2 * hp + h, b * P:(b + 1) * P],
                                   qT[dn % 2][0:KC, j, 2 * hp + h, off:CH], start=True, stop=True)
                mm.then_inc(s_done, 1)

            def products(i, dn, j, b, half):
                n = 2 * i + dn
                off = max(0, b - T * j) * P
                if half == 0 and b == 0:
                    pe.wait_ge(o_read, step_no(n, j))
                    if j == 0:
                        pe.wait_ge(v_ready, n + 1)
                if half == 0 and b < T * j:
                    pe.wait_ge(exp_done, FREE_S + exp_units(n, j, b + 1))
                elif half == 0:
                    pe.wait_ge(diag_done, T * step_no(n, j) + b - T * j + 1)
                cut = CH if b == 0 else max(off, CH // 2)
                start, end = (off, cut) if half == 0 else (cut, CH)
                if start < end:
                    for h in range(G):
                        mm = pe.matmul(o_ps[VW * h:VW * (h + 1), start:end], v_w[dn % 2][:, b, h, :],
                                       probs[:, b % PBUF, h, start:end], start=(b == 0), stop=(b == T * j + T - 1))
                    if end == CH:
                        mm.then_inc(pv_done, 1)

            def body(i, dn, j, final):
                last = T * j + T
                for b in range(last):
                    x = key_blocks(0, j, b)
                    aheads = (0, 1) if exists(i, dn + 1) else (0,)
                    units = [(ahead, u) for ahead in aheads for u in unit_slots.get(x - SLOTS * ahead, [])]
                    turns = [(ahead, m) for ahead, m in due(turn_slots, x) if ahead in aheads]

                    def some(quarter):
                        for ahead, u in units[len(units) * quarter // 4:len(units) * (quarter + 1) // 4]:
                            find(i, dn + ahead, u)

                    some(0)
                    scores(i, dn, j, b, 0)
                    some(1)
                    scores(i, dn, j, b, 1)
                    some(2)
                    for ahead, m in turns:
                        turn_max(i, dn + ahead, m)
                    for half in range(2):
                        if b >= 2:
                            products(i, dn, j, b - 2, half)
                        elif (dn, j) != (0, 0):
                            pdn, pj = preceding(dn, j)
                            products(i, pdn, pj, T * pj + T - 2 + b, half)
                        if half == 0:
                            some(3)
                    if b == SUM and (dn, j) != (0, 0):
                        turn_sum(i, *preceding(dn, j))
                if final:
                    for b in (last - 2, last - 1):
                        for half in range(2):
                            products(i, dn, j, b, half)
                    turn_sum(i, dn, j, True)

            pe.wait_ge(const_ok, 2)
            pe.wait_ge(ones_ok, 6)
            for x in range(MAX_FROM, 0):
                for u in unit_slots[x]:
                    find(0, 0, u)
                if x in turn_slots:
                    turn_max(0, 0, turn_slots[x])
            steps(pe, body)


def build(nc, x, w, out):
    x1 = nc.dram_tensor("x1", (TOK, E), F32, kind="Internal").ap()
    v = nc.dram_tensor("v_tok", (TOK, E), F32, kind="Internal").ap()
    qkT = nc.dram_tensor("qkT_parts", (3, 2 * E, TOK), BF16, kind="Internal").ap()
    attn = nc.dram_tensor("attn_tok", (TOK, E), F32, kind="Internal").ap()
    ffn_phase(nc, True, x, x1, w, {"v": v, "qkT": qkT})
    attention_phase(nc, w, {"v": v, "qkT": qkT, "attn": attn})
    ffn_phase(nc, False, x1, out, w, {"attn": attn})


def kernel(L0_attn_x, L0_attn_Wq, L0_attn_Wk, L0_attn_Wv, L0_attn_bv, L0_attn_Wo, L0_attn_bo, L0_ffn_W_fc,
           L0_ffn_W_proj):
    import numpy as np
    import concourse.bacc as bacc
    from concourse.bass_utils import run_bass_kernel_spmd

    f32 = np.float32
    inv = (f32(1.0) / f32(10000.0) ** (np.arange(0, D, 2, dtype=f32) / f32(D))).astype(f32)
    angle = np.arange(S, dtype=f32)[:, None] * inv[None, :]
    scale = f32(D ** -0.5)

    def table(t):
        return np.tile(np.concatenate([t * scale, t], axis=1).astype(f32), (B, 1))

    arrays = {
        "x": np.asarray(L0_attn_x).reshape(TOK, E),
        "up": np.asarray(L0_ffn_W_fc).T,
        "down": np.asarray(L0_ffn_W_proj).T,
        "qkv": np.concatenate([np.asarray(L0_attn_Wq).T, np.asarray(L0_attn_Wk).T, np.asarray(L0_attn_Wv).T], axis=1),
        "o": np.asarray(L0_attn_Wo).T,
        "bv": np.asarray(L0_attn_bv),
        "bo": np.asarray(L0_attn_bo),
        "cos": table(np.cos(angle)),
        "sin": table(np.sin(angle)),
        "ident": np.eye(P, dtype=f32),
        "mask": np.triu(np.full((P, P), NEG, dtype=f32), k=1),
    }
    arrays = {k: np.ascontiguousarray(a) for k, a in arrays.items()}
    nc = bacc.Bacc("TRN2", target_bir_lowering=False, num_devices=1)
    w = {k: nc.dram_tensor(f"in_{k}", a.shape, F32, kind="ExternalInput").ap() for k, a in arrays.items()}
    out = nc.dram_tensor("out", (TOK, E), F32, kind="ExternalOutput").ap()
    build(nc, w["x"], w, out)
    r = run_bass_kernel_spmd(nc, [{f"in_{k}": a for k, a in arrays.items()}], core_ids=[0])
    return r.results[0]["out"].reshape(B, S, E)
```

```python
import concourse.bass as bass
from concourse import mybir
from contextlib import ExitStack

F32 = mybir.dt.float32
F32R = mybir.dt.float32r
BF16 = mybir.dt.bfloat16
ALU = mybir.AluOpType
ACT = mybir.ActivationFunctionType
AX = mybir.AxisListType

P = 128
E = 256
EC = E // P
F = 1024
FC = F // P
B = 2
S = 2048
TOK = B * S
CH = 512
T = CH // P
NC = TOK // CH
H = 16
D = 16
G = 4
NG = H // G
EPS = 1e-5
BETA = 0.9
THRESHOLD = 1.0
STEPS = 5
HB = 4
LAG = 2
QS, KS = (0, 0, 1, 1, 0, 2), (0, 1, 0, 1, 2, 0)
NT = len(QS)
KR = NT * D
KC = KR + 3
NEG = -3.0e38


def ffn_phase(nc, first, src, dst, w, io, shared):
    tag = "a" if first else "c"
    with ExitStack() as ctx:
        def sb(name, shape, dt=F32):
            return ctx.enter_context(nc.sbuf_tensor(f"{name}_{tag}", shape, dt))

        def pb(name, shape, dt=F32):
            return ctx.enter_context(nc.psum_tensor(f"{name}_{tag}", shape, dt))

        def sem(name):
            return ctx.enter_context(nc.semaphore(f"{name}_{tag}"))

        PN = 3 * E if first else E
        up_hi, up_lo, down_hi, down_lo = shared
        proj_hi, proj_lo = sb("proj_hi", [P, EC, PN], F32R), sb("proj_lo", [P, EC, PN], F32R)
        ident, identb = sb("ident", [P, P]), sb("identb", [P, P], BF16)
        bias = sb("bias", [P, E])

        xin = sb("xin", [P, T, E])
        xn = sb("xn", [P, T, E])
        xT_hi, xT_lo = sb("xT_hi", [P, EC, CH], F32R), sb("xT_lo", [P, EC, CH], F32R)
        mT_hi, mT_lo = sb("mT_hi", [P, EC, CH], F32R), sb("mT_lo", [P, EC, CH], F32R)
        stats, mv, ln = sb("stats", [P, T, 6]), sb("mv", [P, T, 2]), sb("ln", [P, 6, T])
        relu, hsq = sb("relu", [P, 2, CH]), sb("hsq", [P, 2, CH])
        h_hi, h_lo = sb("h_hi", [P, HB, CH], F32R), sb("h_lo", [P, HB, CH], F32R)
        y = sb("y", [P, EC, CH])
        mem, part = sb("mem", [P, 2, EC, CH]), sb("part", [P, EC, CH])
        count = sb("count", [P, EC, CH], BF16)
        xres = sb("xres", [P, T, E])
        xsum = sb("xsum", [P, T, E])
        if first:
            xm = sb("xm", [P, T, E])
            mstats, mmv, mln = sb("mstats", [P, T, 6]), sb("mmv", [P, T, 2]), sb("mln", [P, 6, T])
            qk, rq, rest = (sb(n, [P, T, 2 * E]) for n in ("qk", "rq", "rest"))
            prod = sb("prod", [P, 4, E])
            parts = sb("parts", [P, T, 3, 2 * E], BF16)
            qkT = sb("qkT", [P, 12, CH], BF16)
            v = sb("v", [P, T, E])
            cosb, sinb = sb("cosb", [P, TOK // P, 2, D // 2]), sb("sinb", [P, TOK // P, 2, D // 2])
            staged = [rest[:, :, :].rearrange("p t n -> p (t n)"), qk[:, :, :].rearrange("p t n -> p (t n)"),
                      rq[:, 0:3, :].rearrange("p t n -> p (t n)")]
            split = list(zip(("up", "down", "qkv"), staged, (up_hi, down_hi, proj_hi), (up_lo, down_lo, proj_lo)))
        else:
            ain = sb("ain", [P, T, E])
            xb, x2 = sb("xb", [P, T, E]), sb("x2", [P, T, E])
            split = [("o", sb("stage_o", [P, EC * E])[:, :], proj_hi, proj_lo)]

        tps, yps = pb("tps", [P, EC, CH]), pb("yps", [P, EC, CH])
        ups, gps = pb("ups", [P, 2, CH]), pb("gps", [P, 2, CH])
        gpsb = [gps[:, g, :].bitcast(BF16) for g in range(2)]
        counts = (tps if first else gps)[:, 0, :].bitcast(BF16)

        norm_steps = ("stats", "aggr", "var", "std", "rec", "sq", "err", "fix", "rstd", "norm", "T", "hi", "evac")
        names = ["w_in_" + n for n, _, _, _ in split]
        names += ["const_in", "w_hi", "w_lo", "identb_ok", "x_in", "res_in", "up_done", "relu_done", "hi_done",
                  "sq_done", "lo_done", "down_done", "y_evac", "spike", "count_T", "sum_done", "sum_out"]
        names += ["pre_" + n for n in norm_steps]
        if first:
            names += ["mid_" + n for n in norm_steps]
            names += ["qk_done", "qk_evac", "v_done", "v_evac", "v_out", "rope_mul", "rope_done",
                      "p0_done", "p1_done", "rest_done", "p2_done", "fill_done", "fill_evac", "qkT_out0", "qkT_out1"]
        else:
            names += ["a_in", "a_T", "a_hi", "a_evac", "o_done", "xb_done", "x2_done", "x2_out"]
        s = {n: sem(n) for n in names}
        passed, passed_dve, passed_sp = sem("passed"), sem("passed_dve"), sem("passed_sp")
        CONSTS = 16 * (4 if first else 2)
        SP = 3 * (STEPS - 1) + 1
        SPIKES = {2: 2, 3: 1, 4: 1, 5: 1, 6: 1, 7: 2, 0: 3, 1: 2} if first else {2: 2, 3: 1, 4: 2, 5: 0, 6: 1, 7: 2, 0: 3, 1: 2}
        FILLS = 2 * T
        FB = 12 // 2

        def rows(ap, c):
            return ap[bass.ds(c * CH, CH), :].rearrange("(t p) e -> p t e", p=P)

        def wait(eng, name, value):
            if not isinstance(value, int) or value > 0:
                eng.wait_ge(s[name], value)

        def pipeline(eng, body):
            lo, hi, end = (5, NC - 1, NC + 5) if first else (3, NC - 1, NC + 3)
            for n in range(lo):
                body(n, lambda k: 0 <= n - k < NC)
            with eng.Fori(lo, hi) as it:
                body(it, lambda k: True)
            for n in range(hi, end):
                body(n, lambda k: 0 <= n - k < NC)

        block = ctx.enter_context(nc.Block())

        @block.sync
        def _(sp):
            def load_weight(i):
                name, st, _, _ = split[i]
                sp.dma_start(st.rearrange("p (c n) -> p c n", n=w[name].shape[1]),
                             w[name].rearrange("(c p) n -> p c n", p=P)).then_inc(s["w_in_" + name], 16)

            if first:
                sp.dma_start(xin[:, :, :], rows(src, 0)).then_inc(s["x_in"], 16)
                load_weight(0)
            else:
                sp.dma_start(ain[:, :, :], rows(io["attn"], 0)).then_inc(s["a_in"], 16)
                load_weight(0)
                sp.dma_start(xin[:, :, :], rows(src, 0)).then_inc(s["x_in"], 16)
            sp.dma_start(ident[:, :], w["ident"]).then_inc(s["const_in"], 16)
            sp.dma_start(bias[:, :], w["bv" if first else "bo"].partition_broadcast(P)).then_inc(s["const_in"], 16)
            if first:
                for tab, name in ((cosb, "cos"), (sinb, "sin")):
                    sp.dma_start(tab[:, :, :, :], w[name].rearrange("(t p) (k i) -> p t k i", p=P, k=2))\
                      .then_inc(s["const_in"], 16)
                load_weight(1)
                load_weight(2)

            def hold(name, value):
                if not isinstance(value, int) or value > 0:
                    sp.wait_ge(s[name], value)
                    if not isinstance(value, int):
                        sp.sem_inc(passed_sp, 1)

            def store_parts(c, half):
                hold("fill_evac", FILLS * c + T * (half + 1))
                n = CH // 2
                for a in range(3):
                    sp.dma_start(io["qkT"][a].rearrange("(k p) n -> p k n", p=P)[:, :, bass.ds(c * CH + half * n, n)],
                                 qkT[:, 4 * a:4 * a + 4, half * n:(half + 1) * n]).then_inc(s[f"qkT_out{half}"], 16)

            def body(it, has):
                if has(-1):
                    if first:
                        hold("pre_norm", it + 1)
                    else:
                        hold("a_T", it + 1)
                        sp.dma_start(ain[:, :, :], rows(io["attn"], it + 1)).then_inc(s["a_in"], 16)
                        hold("xb_done", it + 1)
                    sp.dma_start(xin[:, :, :], rows(src, it + 1)).then_inc(s["x_in"], 16)
                if has(2):
                    hold("sum_done", it - 2)
                    if not first:
                        hold("x2_out", 16 * (it - 1))
                    sp.dma_start(xres[:, :, :], rows(src if first else io["x2"], it - 2)).then_inc(s["res_in"], 16)
                if first and has(4):
                    store_parts(it - 4, 1)
                if has(2):
                    hold("sum_done", it - 1)
                    sp.dma_start(rows(dst, it - 2), xsum[:, :, :]).then_inc(s["sum_out"], 16)
                if not first and has(-1):
                    hold("x2_done", it + 2)
                    sp.dma_start(rows(io["x2"], it + 1), x2[:, :, :]).then_inc(s["x2_out"], 16)
                if first and has(3):
                    hold("v_evac", T * (it - 2))
                    sp.dma_start(rows(io["v"], it - 3), v[:, :, :]).then_inc(s["v_out"], 16)
                    store_parts(it - 3, 0)

            if not first:
                wait(sp, "x2_done", 1)
                sp.dma_start(rows(io["x2"], 0), x2[:, :, :]).then_inc(s["x2_out"], 16)
            pipeline(sp, body)
            wait(sp, "sum_out", 16 * NC)
            if first:
                wait(sp, "v_out", 16 * NC)
                wait(sp, "qkT_out0", 48 * NC)
                wait(sp, "qkT_out1", 48 * NC)
            else:
                wait(sp, "x2_out", 16 * NC)

        @block.scalar
        def _(act):
            def std(which, c, l):
                wait(act, which + "_var", c + 1)
                act.activation(l[:, 1, :], l[:, 0, :], ACT.Sqrt).then_inc(s[which + "_std"], 1)

            def high(which, c, hi):
                wait(act, which + "_T", c + 1)
                act.activation(hi[:, :, :], tps[:, :, :], ACT.Copy).then_inc(s[which + "_hi"], 1)

            def fill_evac(c, i):
                t, half = divmod(i, 2)
                wait(act, "fill_done", FILLS * c + i + 1)
                if i in (0, T):
                    wait(act, f"qkT_out{i // T}", 48 * c)
                act.activation(qkT[:, FB * half:FB * (half + 1), t * P:(t + 1) * P],
                               gpsb[1][:, 0:FB * P].rearrange("p (k n) -> p k n", k=FB), ACT.Copy)\
                    .then_inc(s["fill_evac"], 1)

            def part(c, t, k):
                if k == 0:
                    wait(act, "rope_done", 2 * (T * c + t + 1))
                    wait(act, "fill_done", FILLS * (c - 1) + 2 * t + 2)
                    act.activation(parts[:, t, 0, :], rq[:, t, :], ACT.Copy).then_inc(s["p0_done"], 1)
                else:
                    wait(act, "rest_done", T * c + t + 1)
                    act.activation(parts[:, t, 1, :], rest[:, t, :], ACT.Copy).then_inc(s["p1_done"], 1)

            def body(it, has):
                for f in range(FC):
                    if f == LAG and has(1):
                        wait(act, "down_done", FC * it)
                        wait(act, "spike", SP * (it - 1))
                        act.activation(y[:, :, :], yps[:, :, :], ACT.Copy).then_inc(s["y_evac"], 1)
                    if has(0):
                        n = it * FC + f
                        wait(act, "up_done", n + 1)
                        wait(act, "sq_done", n - 1)
                        act.activation(relu[:, f % 2, :], ups[:, f % 2, :], ACT.Relu).then_inc(s["relu_done"], 1)
                        wait(act, "relu_done", n + 1)
                        wait(act, "down_done", n - HB + 1)
                        act.activation(h_hi[:, f % HB, :], relu[:, f % 2, :], ACT.Square).then_inc(s["hi_done"], 1)
                    if not first and has(-1) and f == 2:
                        wait(act, "o_done", it + 1)
                        high("a", it + 1, mT_hi)
                    if first and has(2) and f == 3:
                        std("mid", it - 2, mln)
                    if has(-1) and f == 5:
                        std("pre", it + 1, ln)
                    if has(-1) and f == 7:
                        wait(act, "up_done", FC * it + FC)
                        high("pre", it + 1, xT_hi)
                    if first and f == 5 and has(2):
                        wait(act, "v_done", T * (it - 2))
                        high("mid", it - 2, mT_hi)
                    if first:
                        if f % 2 == 1 and has(3):
                            part(it - 3, f // 2, 0)
                        k = 3 if f else 4
                        if f % 2 == 0 and has(k):
                            part(it - k, (f // 2 - 1) % T, 1)
                        k = 2 if f == 6 else 3
                        if f % 2 == 0 and has(k):
                            c, t = it - k, ((f - 6) % FC) // 2
                            wait(act, "qk_done", T * c + t + 1)
                            wait(act, "rope_done", 2 * (T * (c - 1) + t + 1))
                            act.activation(qk[:, t, :], gps[:, 0, :], ACT.Copy).then_inc(s["qk_evac"], 1)
                        k = 3 if f >= 3 else 4
                        if has(k):
                            fill_evac(it - k, (f - 3) % FC)

            for name, st, hi, _ in split:
                act.wait_ge(s["w_in_" + name], 16)
                act.activation(hi[:, :, :].rearrange("p c n -> p (c n)"), st, ACT.Copy).then_inc(s["w_hi"], 1)
                if name in ("up", "o"):
                    act.wait_ge(s["const_in"], CONSTS)
                    act.activation(identb[:, :], ident[:, :], ACT.Copy).then_inc(s["identb_ok"], 1)
                    if not first:
                        high("a", 0, mT_hi)
                    std("pre", 0, ln)
                    high("pre", 0, xT_hi)
            pipeline(act, body)

        @block.vector
        def _(dve):
            def norm_stats(which, c, x, st, m, l):
                for t in range(T):
                    dve.bn_stats(st[:, t, :], x[:, t, :]).then_inc(s[which + "_stats"], 1)
                wait(dve, which + "_stats", T * c + T)
                dve.sem_inc(passed_dve, 1)
                for t in range(T):
                    dve.bn_aggr(m[:, t, :], st[:, t, :]).then_inc(s[which + "_aggr"], 1)
                wait(dve, which + "_aggr", T * c + T)
                dve.tensor_scalar(l[:, 0, :], m[:, :, 1], EPS, None, ALU.add).then_inc(s[which + "_var"], 1)

            def norm(which, c, x, o, m, l):
                wait(dve, which + "_std", c + 1)
                dve.reciprocal(l[:, 2, :], l[:, 1, :]).then_inc(s[which + "_rec"], 1)
                wait(dve, which + "_rec", c + 1)
                dve.tensor_tensor(l[:, 3, :], l[:, 2, :], l[:, 2, :], ALU.mult).then_inc(s[which + "_sq"], 1)
                wait(dve, which + "_sq", c + 1)
                dve.tensor_tensor(l[:, 4, :], l[:, 3, :], l[:, 0, :], ALU.mult).then_inc(s[which + "_err"], 1)
                wait(dve, which + "_err", c + 1)
                dve.tensor_scalar(l[:, 5, :], l[:, 4, :], -0.5, 1.5, ALU.mult, ALU.add).then_inc(s[which + "_fix"], 1)
                wait(dve, which + "_fix", c + 1)
                dve.tensor_tensor(l[:, 3, :], l[:, 2, :], l[:, 5, :], ALU.mult).then_inc(s[which + "_rstd"], 1)
                wait(dve, which + "_rstd", c + 1)
                wait(dve, which + "_T", c)
                for t in range(T):
                    last = dve.tensor_scalar(o[:, t, :], x[:, t, :], m[:, t, 0:1], l[:, 3, t:t + 1],
                                             ALU.subtract, ALU.mult)
                last.then_inc(s[which + "_norm"], 1)

            def low(which, c, hi, lo):
                wait(dve, which + "_hi", c + 1)
                dve.tensor_tensor(lo[:, :, :], tps[:, :, :], hi[:, :, :].bitcast(F32), ALU.subtract)\
                   .then_inc(s[which + "_evac"], 1)

            def spikes(c, k0, k1):
                for k in range(k0, k1):
                    step, what = (k - 1) // 3, (k - 1) % 3
                    cur, sign, above = (y, 1.0, ALU.is_gt) if step == 0 else (mem[:, (step - 1) % 2], -1.0, ALU.is_lt)
                    cur = cur[:, :, :] if step == 0 else cur
                    if k == 0:
                        wait(dve, "y_evac", c + 1)
                        wait(dve, "count_T", c)
                        dve.tensor_scalar(count[:, :, :], y[:, :, :], THRESHOLD, None, ALU.is_gt)\
                           .then_inc(s["spike"], 1)
                        continue
                    wait(dve, "spike", SP * c + k)
                    if what == 0:
                        dve.scalar_tensor_tensor(out=part[:, :, :], in0=cur, scalar=sign * BETA, in1=y[:, :, :],
                                                 op0=ALU.mult, op1=ALU.add).then_inc(s["spike"], 1)
                    elif what == 1:
                        dve.scalar_tensor_tensor(out=mem[:, step % 2], in0=cur, scalar=sign * THRESHOLD,
                                                 in1=part[:, :, :], op0=above, op1=ALU.subtract)\
                           .then_inc(s["spike"], 1)
                    else:
                        dve.scalar_tensor_tensor(out=count[:, :, :], in0=mem[:, step % 2], scalar=-THRESHOLD,
                                                 in1=count[:, :, :], op0=ALU.is_lt, op1=ALU.add)\
                           .then_inc(s["spike"], 1)

            def sum_(c):
                wait(dve, "count_T", c + 1)
                wait(dve, "res_in", 16 * (c + 1))
                wait(dve, "sum_out", 16 * c)
                dve.scalar_tensor_tensor(out=xsum[:, :, :].rearrange("p t e -> p (t e)"), in0=counts,
                                         scalar=0.5 / STEPS, in1=xres[:, :, :].rearrange("p t e -> p (t e)"),
                                         op0=ALU.mult, op1=ALU.add).then_inc(s["sum_done"], 1)

            def attn_sum(c):
                wait(dve, "o_done", c + 1)
                wait(dve, "xb_done", c + 1)
                wait(dve, "x2_out", 16 * c)
                dve.tensor_tensor(x2[:, :, :].rearrange("p t e -> p (t e)"), gps[:, :, :].rearrange("p g n -> p (g n)"),
                                  xb[:, :, :].rearrange("p t e -> p (t e)"), ALU.add).then_inc(s["x2_done"], 1)
                wait(dve, "x2_done", c + 1)

            def body(it, has):
                for f in range(FC):
                    before = sum(SPIKES[x % FC] for x in range(LAG, f + FC * (f < LAG)))
                    k = 1 if f >= LAG else 2
                    if first and f == 6 and has(2):
                        low("mid", it - 2, mT_hi, mT_lo)
                    if not first and f == 3 and has(-1):
                        low("a", it + 1, mT_hi, mT_lo)
                    if f == 3 and has(2):
                        sum_(it - 2)
                    if f != 2 and has(k):
                        spikes(it - k, before, before + SPIKES[f])
                    if has(0):
                        n = it * FC + f
                        wait(dve, "sq_done", n + 1)
                        wait(dve, "hi_done", n + 1)
                        wait(dve, "down_done", n - HB + 1)
                        dve.tensor_tensor(h_lo[:, f % HB, :], hsq[:, f % 2, :], h_hi[:, f % HB, :].bitcast(F32),
                                          ALU.subtract).then_inc(s["lo_done"], 1)
                    if f == 2 and has(k):
                        spikes(it - k, before, before + SPIKES[f])
                    if first:
                        if f == 3 and has(2):
                            wait(dve, "sum_done", it - 1)
                            norm_stats("mid", it - 2, xsum, mstats, mmv, mln)
                        if f == 4 and has(2):
                            norm("mid", it - 2, xsum, xm, mmv, mln)
                        if f == 5 and has(-1):
                            wait(dve, "x_in", 16 * (it + 2))
                            norm_stats("pre", it + 1, xin, stats, mv, ln)
                        if f == 6 and has(-1):
                            norm("pre", it + 1, xin, xn, mv, ln)
                        if f % 2 == 1 and has(3):
                            c, t = it - 3, f // 2
                            wait(dve, "p0_done", T * c + t + 1)
                            dve.tensor_tensor(rest[:, t, :], rq[:, t, :], parts[:, t, 0, :], ALU.subtract)\
                               .then_inc(s["rest_done"], 1)
                        q = 3 if f else 4
                        if f % 2 == 0 and has(q):
                            c, t = it - q, (f // 2 - 1) % T
                            wait(dve, "p1_done", T * c + t + 1)
                            dve.tensor_tensor(parts[:, t, 2, :], rest[:, t, :], parts[:, t, 1, :], ALU.subtract)\
                               .then_inc(s["p2_done"], 1)
                    elif has(-1):
                        if f == 5:
                            attn_sum(it + 1)
                            norm_stats("pre", it + 1, x2, stats, mv, ln)
                        if f == 6:
                            norm("pre", it + 1, x2, xn, mv, ln)
                    if f == 7 and has(-1):
                        low("pre", it + 1, xT_hi, xT_lo)
                    q = 2 if f == 7 else 3
                    if first and f % 2 == 1 and has(q):
                        c, t = it - q, ((f - 7) % FC) // 2
                        wait(dve, "v_done", T * c + t + 1)
                        wait(dve, "v_out", 16 * c)
                        dve.tensor_tensor(v[:, t, :], gps[:, 0, 0:E], bias[:, :], ALU.add).then_inc(s["v_evac"], 1)

            def split_low(i):
                _, st, hi, lo = split[i]
                dve.wait_ge(s["w_hi"], i + 1)
                dve.tensor_tensor(lo[:, :, :].rearrange("p c n -> p (c n)"), st,
                                  hi[:, :, :].rearrange("p c n -> p (c n)").bitcast(F32), ALU.subtract)\
                   .then_inc(s["w_lo"], 1)

            if first:
                wait(dve, "x_in", 16)
                norm_stats("pre", 0, xin, stats, mv, ln)
                split_low(0)
                norm("pre", 0, xin, xn, mv, ln)
            else:
                split_low(0)
                low("a", 0, mT_hi, mT_lo)
                attn_sum(0)
                norm_stats("pre", 0, x2, stats, mv, ln)
                norm("pre", 0, x2, xn, mv, ln)
            low("pre", 0, xT_hi, xT_lo)
            if first:
                split_low(1)
                split_low(2)
                wait(dve, "const_in", CONSTS)
            pipeline(dve, body)

        @block.gpsimd
        def _(pool):
            def rope(c, t, half):
                n = 2 * (T * c + t) + half
                if half == 0:
                    wait(pool, "qk_evac", T * c + t + 1)
                x = qk[:, t, :].rearrange("p (k h i two) -> p k h i two", k=2, h=H, two=2)
                o = rq[:, t, :].rearrange("p (h i two) -> p h i two", i=D // 2, two=2)

                def table(tab):
                    return tab[:, bass.ds(T * c + t, 1), :, :].rearrange("p o k i -> p (o k) i").unsqueeze(2)\
                        .broadcast_to([P, 2, H, D // 2])

                wait(pool, "rope_done", n - 1)
                pool.sem_inc(passed, 1)
                for m, tab in enumerate((sinb, cosb) if half else (cosb, sinb)):
                    pool.tensor_tensor(prod[:, 2 * half + m, :].rearrange("p (k h i) -> p k h i", k=2, h=H),
                                       x[:, :, :, :, m], table(tab), ALU.mult).then_inc(s["rope_mul"], 1)
                wait(pool, "rope_mul", 2 * n + 2)
                wait(pool, "rest_done", T * (c - 1) + t + 1)
                p4 = prod[:, :, :].rearrange("p n (h i) -> p n h i", i=D // 2)
                pool.tensor_tensor(o[:, :, :, half], p4[:, 2 * half], p4[:, 2 * half + 1],
                                   ALU.add if half else ALU.subtract).then_inc(s["rope_done"], 1)

            def add_bias(c):
                wait(pool, "x_in", 16 * (c + 1))
                wait(pool, "x2_done", c)
                pool.tensor_tensor(xb[:, :, :], xin[:, :, :], bias[:, :].unsqueeze(1).broadcast_to([P, T, E]), ALU.add)\
                    .then_inc(s["xb_done"], 1)

            def body(it, has):
                for f in range(FC):
                    if has(0):
                        n = it * FC + f
                        wait(pool, "relu_done", n + 1)
                        wait(pool, "lo_done", n - 1)
                        pool.tensor_tensor(hsq[:, f % 2, :], relu[:, f % 2, :], relu[:, f % 2, :], ALU.mult)\
                            .then_inc(s["sq_done"], 1)
                    k = 2 if f == 7 else 3
                    if first and has(k):
                        rope(it - k, ((f + 1) % FC) // 2, (f + 1) % 2)
                    if not first and has(-1) and f == 3:
                        add_bias(it + 1)

            wait(pool, "const_in", CONSTS)
            if first:
                wait(pool, "w_lo", 3)
            else:
                add_bias(0)
            pipeline(pool, body)

        @block.tensor
        def _(pe):
            def up(it, f):
                n = it * FC + f
                if f == 0:
                    wait(pe, "pre_evac", it + 1)
                wait(pe, "relu_done", n - 1)
                for i, (wt, x, c) in enumerate([(a, b, c) for c in range(EC) for a, b in
                                                ((up_hi, xT_hi), (up_hi, xT_lo), (up_lo, xT_hi))]):
                    last = pe.matmul(ups[:, f % 2, :], wt[:, c, f * P:(f + 1) * P], x[:, c, :],
                                     start=(i == 0), stop=(i == 3 * EC - 1))
                last.then_inc(s["up_done"], 1)

            def down(it, f):
                if f == 0:
                    wait(pe, "y_evac", it)
                    if first and isinstance(it, int) and it == 0:
                        wait(pe, "w_lo", 2)
                wait(pe, "lo_done", it * FC + f + 1)
                for c in range(EC):
                    for i, (wt, h) in enumerate(((down_hi, h_hi), (down_hi, h_lo), (down_lo, h_hi))):
                        last = pe.matmul(yps[:, c, :], wt[:, f, c * P:(c + 1) * P], h[:, f % HB, :],
                                         start=(f == 0 and i == 0), stop=(f == FC - 1 and i == 2))
                last.then_inc(s["down_done"], 1)

            def turn(x, done):
                for t in range(T):
                    for c in range(EC):
                        last = pe.transpose(tps[:, c, t * P:(t + 1) * P], x[:, t, c * P:(c + 1) * P], ident[:, :])
                last.then_inc(s[done], 1)

            def count_turn(c):
                wait(pe, "spike", SP * (c + 1))
                for t in range(T):
                    for k in range(EC):
                        last = pe.transpose(counts[:, t * E + k * P:t * E + (k + 1) * P],
                                            count[:, k, t * P:(t + 1) * P], identb[:, :])
                last.then_inc(s["count_T"], 1)

            def fill(c, i):
                t, half = divmod(i, 2)
                if half == 0:
                    wait(pe, "p2_done", T * c + t + 1)
                wait(pe, "fill_evac", FILLS * c + i)
                for b in range(FB):
                    a, blk = divmod(FB * half + b, 4)
                    last = pe.transpose(gpsb[1][:, b * P:(b + 1) * P], parts[:, t, a, blk * P:(blk + 1) * P],
                                        identb[:, :])
                last.then_inc(s["fill_done"], 1)

            def project(out, t, c0, c1):
                for i, (wt, x, c) in enumerate([(a, b, c) for c in range(EC) for a, b in
                                                ((proj_hi, mT_hi), (proj_hi, mT_lo), (proj_lo, mT_hi))]):
                    last = pe.matmul(out, x[:, c, t * P:(t + 1) * P], wt[:, c, c0:c1],
                                     start=(i == 0), stop=(i == 3 * EC - 1))
                return last

            def qkv(c, i):
                t = i // 2
                if i == 0:
                    wait(pe, "mid_evac", c + 1)
                if i % 2 == 0:
                    wait(pe, "v_evac", T * c + t)
                    project(gps[:, 0, :], t, 0, 2 * E).then_inc(s["qk_done"], 1)
                else:
                    wait(pe, "qk_evac", T * c + t + 1)
                    project(gps[:, 0, 0:E], t, 2 * E, 3 * E).then_inc(s["v_done"], 1)

            def attn_turn(c):
                wait(pe, "a_in", 16 * (c + 1))
                wait(pe, "pre_evac", c)
                turn(ain, "a_T")

            def attn_out(c):
                wait(pe, "a_evac", c + 1)
                for t in range(T):
                    last = project(gps[:, t // 2, (t % 2) * E:(t % 2 + 1) * E], t, 0, E)
                last.then_inc(s["o_done"], 1)

            def body(it, has):
                for f in range(FC):
                    if f == 2 and has(2):
                        count_turn(it - 2)
                    if f > 0 and has(0):
                        up(it, f)
                    if f == 7 and has(-1):
                        wait(pe, "pre_norm", it + 2)
                        if first and has(2):
                            wait(pe, "mid_evac", it - 1)
                        turn(xn, "pre_T")
                    if not first and f == 2 and has(-1):
                        attn_turn(it + 1)
                    if not first and f == 4 and has(-1):
                        if has(2):
                            wait(pe, "sum_done", it - 1)
                        attn_out(it + 1)
                    k = 0 if f >= LAG else 1
                    if has(k):
                        down(it - k, (f - LAG) % FC)
                    if first:
                        k = 2 if f >= 6 else 3
                        if has(k):
                            qkv(it - k, (f - 6) % FC)
                        if f == 5 and has(2):
                            wait(pe, "mid_norm", it - 1)
                            turn(xm, "mid_T")
                        k = 3 if f >= 3 else 4
                        if has(k):
                            fill(it - k, (f - 3) % FC)
                    if f == 0 and has(0):
                        up(it, 0)

            wait(pe, "const_in", CONSTS)
            wait(pe, "identb_ok", 1)
            if not first:
                attn_turn(0)
                wait(pe, "w_lo", 1)
                attn_out(0)
            wait(pe, "pre_norm", 1)
            turn(xn, "pre_T")
            if first:
                wait(pe, "w_lo", 1)
            pipeline(pe, body)


def attention_phase(nc, w, io):
    with ExitStack() as ctx:
        def sb(name, shape, dt=F32):
            return ctx.enter_context(nc.sbuf_tensor(name, shape, dt))

        def pb(name, shape, dt=F32):
            return ctx.enter_context(nc.psum_tensor(name, shape, dt))

        def sem(name):
            return ctx.enter_context(nc.semaphore(name))

        KB = S // P
        NJ = S // CH
        PAIRS = B * NG // 2
        PBUF = 4
        VW = 32

        qT = [sb(f"qT{p}", [P, NJ, G, CH], BF16) for p in range(2)]
        kT = [sb(f"kT{p}", [P, G, S], BF16) for p in range(2)]
        v_in = [sb(f"v_in{p}", [P, KB, G * D]) for p in range(2)]
        v_w = [sb(f"v_w{p}", [P, KB, G, VW]) for p in range(2)]
        probs = sb("probs", [P, PBUF, G, CH])
        ident, identb = sb("ident_b", [P, P]), sb("identb_b", [P, P], BF16)
        mask, maskb = sb("mask_b", [P, P]), sb("maskb", [P, P], BF16)
        maxes = sb("maxes", [P, 2, G, T, NJ])
        negmax, negrest = sb("negmax", [P, G * T]), sb("negrest", [P, G * T])
        negparts = sb("negparts", [P, P // (G * T), G * T], BF16)
        shiftT = sb("shiftT", [3 * G * T, P], BF16)
        osum = sb("osum", [P, CH])
        denom = sb("denom", [P, T * G])
        att = sb("att", [P, T, G * D])

        s_ps = [pb(f"s_ps{p}", [P, 2, CH]) for p in range(2)]
        m_ps = pb("m_ps", [P, 2, CH])
        o_ps = pb("o_ps", [P, CH])
        t_ps = pb("t_ps", [P, CH])

        const_in, const_ok, ones_ok = sem("const_in_b"), sem("const_ok_b"), sem("ones_ok")
        qk_in = [sem(f"qk_in{p}") for p in range(2)]
        vs_in = [sem(f"vs_in{p}") for p in range(2)]
        v_ready, s_done, exp_done, diag_done, pv_done = (sem(n) for n in (
            "v_ready", "s_done", "exp_done", "diag_done", "pv_done"))
        max_done, max_read, neg_done, neg_step, neg_turned, neg_out, shift_in = (sem(n) for n in (
            "max_done", "max_read", "neg_done", "neg_step", "neg_turned", "neg_out", "shift_in"))
        neg_zero = sem("neg_zero")
        passed = sem("passed_b")
        o_read, o_turned, denom_done, att_done, att_out = (sem(n) for n in (
            "o_read", "o_turned", "denom_done", "att_done", "att_out"))

        def step_no(n, j):
            return NJ * n + j

        def exp_units(n, j, i):
            return 80 * n + 4 * j * (j + 1) + 2 * i

        def key_blocks(n, j, i):
            return 40 * n + 2 * j * (j + 1) + i

        SLOTS = NJ * (NJ + 1) * T // 2
        UNITS = [(j, t, h, k, CH if k < j else P * (t + 1))
                 for j in range(NJ) for t in range(T) for h in range(G) for k in range(j + 1)]
        MAX_FROM, MAX_TO = -20, 20

        def place_units():
            cost = [u[4] + 110 for u in UNITS]
            room = []
            for s in range(MAX_FROM, MAX_TO):
                j, b = [(j, b) for j in range(NJ) for b in range(T * j + T)][s % SLOTS]
                room.append(1 + T - max(0, b - T * j))
            slots, done, full, u = {}, 0, 0, 0
            for s, r in zip(range(MAX_FROM, MAX_TO), room):
                full += r * sum(cost) / sum(room)
                slots[s] = []
                while u < len(UNITS) and (done + cost[u] / 2 <= full):
                    slots[s].append(u)
                    done += cost[u]
                    u += 1
            assert u == len(UNITS)
            return slots

        unit_slots = place_units()
        NEG_OPS = 5

        def vector_items():
            items, pending = {}, []
            for s in sorted(unit_slots):
                items[s] = []
                for u in unit_slots[s]:
                    items[s].append(("unit", u))
                    if u + 1 == len(UNITS) or UNITS[u + 1][0] > UNITS[u][0]:
                        pending = [(UNITS[u][0], k) for k in range(NEG_OPS)]
                    if pending:
                        items[s].append(("negate", pending.pop(0)))
            items[s] += [("negate", x) for x in pending]
            return items

        vector_slots = vector_items()
        found = [max(s for s in vector_slots if ("negate", (m, NEG_OPS - 1)) in vector_slots[s]) for m in range(NJ)]
        SUM = 3
        sum_slots = [2 * j * (j + 1) + SUM for j in range(NJ)]
        turn_slots = {f + 1: m for m, f in enumerate(found)}
        out_slots = {x if x % SLOTS in sum_slots else x + 1: m for x, m in turn_slots.items()}

        def due(slots, s):
            return [(ahead, slots[x]) for ahead, x in ((0, s), (1, s - SLOTS)) if x in slots]

        def turns_before_sum(j):
            return sum(x <= sum_slots[j] for x in turn_slots) + sum(SLOTS + x <= sum_slots[j] for x in turn_slots)

        def sums_before_turn(m):
            x = found[m] + 1
            return sum(y < x for y in sum_slots) - sum(y >= x + SLOTS for y in sum_slots) - 1

        LOADS = 16 * NT * (NJ + 1)
        FREE_P, FREE_S, FREE_M = PBUF, 2, 2

        def wait(eng, sem, value):
            if not isinstance(value, int) or value > 0:
                eng.wait_ge(sem, value)

        def preceding(dn, j):
            return (dn, j - 1) if j else (dn - 1, NJ - 1)

        def exists(i, dn):
            return not isinstance(i, int) or 2 * i + dn < B * NG

        def steps(eng, body):
            turn = [(dn, j) for dn in range(2) for j in range(NJ)][2:] + [(2, 0), (2, 1)]
            body(0, 0, 0, False)
            body(0, 0, 1, False)
            with eng.Fori(0, PAIRS - 1) as i:
                for dn, j in turn:
                    body(i, dn, j, False)
            for dn, j in turn[:-2]:
                body(PAIRS - 1, dn, j, (dn, j) == (1, NJ - 1))

        def place(i, dn):
            i, dn = i + dn // 2, dn % 2
            return (i // 2) * S, ((i % 2) * 2 + dn) * (G * D)

        block = ctx.enter_context(nc.Block())

        @block.sync
        def _(sp):
            sp.dma_start(ident[:, :], w["ident"]).then_inc(const_in, 16)
            sp.dma_start(mask[:, :], w["mask"]).then_inc(const_in, 16)

            def load(i, dn, terms):
                tok, row = place(i, dn)
                p = dn % 2
                for m in terms:
                    q, k = (io["qkT"][a, bass.ds(row + first, G * D), bass.ds(tok, S)] for a, first in
                            ((QS[m], 0), (KS[m], E)))
                    for j in range(NJ):
                        sp.dma_start(qT[p][D * m:D * (m + 1), j, :, :],
                                     q[:, j * CH:(j + 1) * CH].rearrange("(h d) t -> d h t", d=D))\
                          .then_inc(qk_in[p], 16)
                    sp.dma_start(kT[p][D * m:D * (m + 1), :, :], k.rearrange("(h d) t -> d h t", d=D))\
                      .then_inc(qk_in[p], 16)
                    if m == 0:
                        sp.dma_start(v_in[p][:, :, :], io["v"][bass.ds(tok, S), bass.ds(row, G * D)]
                                     .rearrange("(k p) n -> p k n", p=P)).then_inc(vs_in[p], 16)

            def shift(i, dn, j):
                n = 2 * i + dn
                sp.wait_ge(neg_out, step_no(n, j) + 1)
                for a in range(3):
                    sp.dma_start(qT[dn % 2][KR + a:KR + a + 1, j, :, :],
                                 shiftT[a * G * T:(a + 1) * G * T, :]).then_inc(shift_in, 16)

            def body(i, dn, j, final):
                n = 2 * i + dn
                if j < 3 and exists(i, dn + 1):
                    if j == 0 and (dn > 0):
                        sp.wait_ge(s_done, exp_units(n, 0, 0))
                        sp.wait_ge(v_ready, n)
                    load(i, dn + 1, (2 * j, 2 * j + 1))
                for b in range(T * j + T):
                    if b == SUM and (dn, j) != (0, 0):
                        store(i, *preceding(dn, j))
                    for ahead, m in due(out_slots, key_blocks(0, j, b)):
                        if exists(i, dn + ahead):
                            shift(i, dn + ahead, m)
                if final:
                    store(i, dn, j)

            def store(i, dn, j):
                tok, row = place(i, dn)
                sp.wait_ge(att_done, step_no(2 * i + dn, j) + 1)
                sp.dma_start(io["attn"][bass.ds(tok + j * CH, CH), bass.ds(row, G * D)]
                             .rearrange("(t p) n -> p t n", p=P), att[:, :, :]).then_inc(att_out, 16)

            load(0, 0, range(NT))
            for x in range(MAX_FROM, 0):
                if x in out_slots:
                    shift(0, 0, out_slots[x])
            steps(sp, body)
            sp.wait_ge(att_out, 16 * NJ * B * NG)

        @block.gpsimd
        def _(pool):
            for p in range(2):
                pool.memset(kT[p][KR:KC, :, :], 1.0).then_inc(ones_ok, 1)
                pool.wait_ge(ones_ok, 3 * p + 1)
                pool.memset(v_w[p][:, :, :, :], 0.0).then_inc(ones_ok, 1)
                pool.wait_ge(ones_ok, 3 * p + 2)
                pool.memset(v_w[p][:, :, :, D:D + 1], 1.0).then_inc(ones_ok, 1)
                pool.wait_ge(ones_ok, 3 * p + 3)

            def body(i, dn, j, final):
                n = 2 * i + dn
                for a in range(T):
                    pool.wait_ge(exp_done, FREE_S + exp_units(n, j, T * j + a + 1))
                    tile = probs[:, (T * j + a) % PBUF, :, P * a:P * (a + 1)]
                    pool.sem_inc(passed, 1)
                    pool.affine_select(out=tile, in_=tile, compare_op=ALU.is_ge, fill=0.0, base=0,
                                       pattern=[[0, G], [1, P]], channel_multiplier=-1).then_inc(diag_done, 1)

            steps(pool, body)

        @block.scalar
        def _(act):
            act.sem_inc(exp_done, FREE_S)
            act.wait_ge(const_in, 32)
            act.activation(identb[:, :], ident[:, :], ACT.Copy).then_inc(const_ok, 1)
            act.activation(maskb[:, :], mask[:, :], ACT.Copy).then_inc(const_ok, 1)

            def widen(i, dn):
                act.wait_ge(vs_in[dn % 2], 16 * (i + dn // 2 + 1))
                act.activation(v_w[dn % 2][:, :, :, 0:D].rearrange("p k h d -> p (k h) d"),
                               v_in[dn % 2][:, :, :].rearrange("p k (h d) -> p (k h) d", d=D), ACT.Copy)\
                    .then_inc(v_ready, 1)

            def read_sum(i, dn, j):
                n = 2 * i + dn
                act.wait_ge(pv_done, FREE_P + key_blocks(n, j, T * j + T))
                act.wait_ge(o_turned, step_no(n, j))
                act.activation(osum[:, :], o_ps[:, :], ACT.Copy).then_inc(o_read, 1)

            def body(i, dn, j, final):
                n = 2 * i + dn
                for b in range(T * j + T):
                    off = max(0, b - T * j) * P
                    act.wait_ge(pv_done, key_blocks(n, j, b) + 1)
                    for hp in range(2):
                        act.wait_ge(s_done, exp_units(n, j, b) + hp + 1)
                        act.activation(probs[:, b % PBUF, 2 * hp:2 * hp + 2, off:CH], s_ps[hp][:, :, off:CH], ACT.Exp)\
                           .then_inc(exp_done, 1)
                    if b == 1 and (dn, j) != (0, 0):
                        read_sum(i, *preceding(dn, j))
                if j == 1 and exists(i, dn + 1):
                    widen(i, dn + 1)
                if final:
                    read_sum(i, dn, j)

            act.wait_ge(ones_ok, 6)
            widen(0, 0)
            steps(act, body)

        @block.vector
        def _(dve):
            dve.sem_inc(max_read, FREE_M)
            dve.memset(negparts[:, :, :], 0.0).then_inc(neg_zero, 1)
            dve.wait_ge(neg_zero, 1)

            def unit(i, dn, u):
                n = 2 * i + dn
                j, t, h, k, width = UNITS[u]
                dve.wait_ge(max_done, len(UNITS) * n + u + 1)
                dve.tensor_reduce(maxes[:, j % 2, h, t, k:k + 1], m_ps[:, u % 2, 0:width], AX.X, ALU.max)\
                   .then_inc(max_read, 1)

            def negate(i, dn, j, k):
                n = 2 * i + dn
                t = step_no(n, j)
                if k == 0:
                    dve.wait_ge(max_read, FREE_M + len(UNITS) * n + 8 * (j + 1) * (j + 2))
                    dve.tensor_reduce(negmax[:, :], maxes[:, j % 2, :, :, 0:j + 1].rearrange("p h t k -> p (h t) k"), AX.X,
                                      ALU.max, negate=True).then_inc(neg_step, 1)
                elif k == 1:
                    dve.wait_ge(neg_step, 4 * t + 1)
                    wait(dve, neg_turned, t)
                    dve.tensor_copy(negparts[:, 0, :], negmax[:, :]).then_inc(neg_step, 1)
                elif k == 2:
                    dve.wait_ge(neg_step, 4 * t + 2)
                    dve.tensor_tensor(negrest[:, :], negmax[:, :], negparts[:, 0, :], ALU.subtract).then_inc(neg_step, 1)
                elif k == 3:
                    dve.wait_ge(neg_step, 4 * t + 3)
                    dve.tensor_copy(negparts[:, 1, :], negrest[:, :]).then_inc(neg_step, 1)
                else:
                    dve.wait_ge(neg_step, 4 * t + 4)
                    dve.tensor_tensor(negparts[:, 2, :], negrest[:, :], negparts[:, 1, :], ALU.subtract)\
                       .then_inc(neg_done, 1)

            def send(i, dn, j):
                t = step_no(2 * i + dn, j)
                dve.wait_ge(neg_turned, t + 1)
                wait(dve, shift_in, 48 * t)
                dve.tensor_copy(shiftT[:, :], t_ps[:, 0:P // 2].bitcast(BF16)[0:3 * G * T, :]).then_inc(neg_out, 1)

            def normalise(i, dn, j):
                n = 2 * i + dn
                t = step_no(n, j)
                dve.wait_ge(o_turned, t + 1)
                sums = t_ps[:, :].rearrange("p (g w) -> p g w", w=VW)
                dve.reciprocal(denom[:, :].unsqueeze(2), sums[:, :, D:D + 1]).then_inc(denom_done, 1)
                dve.wait_ge(denom_done, t + 1)
                dve.wait_ge(att_out, 16 * t)
                dve.tensor_tensor(att[:, :, :].rearrange("p t (h d) -> p (t h) d", d=D), sums[:, :, 0:D],
                                  denom[:, :].unsqueeze(2).broadcast_to([P, T * G, D]), ALU.mult)\
                   .then_inc(att_done, 1)

            def slot(i, dn, x, ahead):
                for kind, what in vector_slots.get(x, []):
                    if kind == "unit":
                        unit(i, dn + ahead, what)
                    else:
                        negate(i, dn + ahead, *what)
                if x in out_slots:
                    send(i, dn + ahead, out_slots[x])

            def body(i, dn, j, final):
                for b in range(T * j + T):
                    x = key_blocks(0, j, b)
                    slot(i, dn, x, 0)
                    if exists(i, dn + 1):
                        slot(i, dn, x - SLOTS, 1)
                    if b == SUM and (dn, j) != (0, 0):
                        normalise(i, *preceding(dn, j))
                if final:
                    normalise(i, dn, j)

            for x in range(MAX_FROM, 0):
                slot(0, 0, x, 0)
            steps(dve, body)

        @block.tensor
        def _(pe):
            pe.sem_inc(pv_done, FREE_P)

            def find(i, dn, u):
                n = 2 * i + dn
                j, t, h, k, width = UNITS[u]
                if u == 0:
                    pe.wait_ge(qk_in[dn % 2], LOADS * (i + dn // 2 + 1))
                pe.wait_ge(max_read, len(UNITS) * n + u + 1)
                q = qT[dn % 2][0:KR, j, h, t * P:(t + 1) * P]
                mm = pe.matmul(m_ps[:, u % 2, 0:width], q, kT[dn % 2][0:KR, h, k * CH:k * CH + width],
                               start=True, stop=(k < j))
                if k == j:
                    mm = pe.matmul(m_ps[:, u % 2, width - P:width], identb[:, :], maskb[:, :], start=False, stop=True)
                mm.then_inc(max_done, 1)

            def turn_max(i, dn, j):
                n = 2 * i + dn
                wait(pe, att_done, NJ * n + sums_before_turn(j))
                wait(pe, neg_out, step_no(n, j))
                pe.wait_ge(neg_done, step_no(n, j) + 1)
                pe.transpose(t_ps[:, 0:P // 2].bitcast(BF16), negparts[:, :, :].rearrange("p a c -> p (a c)"),
                             identb[:, :]).then_inc(neg_turned, 1)

            def turn_sum(i, dn, j, final=False):
                n = 2 * i + dn
                wait(pe, att_done, step_no(n, j))
                turned = NJ * (n + (j + 1) // NJ) + turns_before_sum((j + 1) % NJ)
                if exists(i, dn + 1):
                    pe.wait_ge(neg_out, turned)
                else:
                    pe.wait_ge(neg_out, min(turned, NJ * B * NG))
                pe.wait_ge(o_read, step_no(n, j) + 1)
                for t in range(T):
                    mm = pe.transpose(t_ps[:, t * P:(t + 1) * P], osum[:, t * P:(t + 1) * P], ident[:, :])
                mm.then_inc(o_turned, 1)

            def scores(i, dn, j, b, hp):
                n = 2 * i + dn
                off = max(0, b - T * j) * P
                if b == 0 and hp == 0:
                    pe.wait_ge(shift_in, 48 * (step_no(n, j) + 1))
                pe.wait_ge(exp_done, exp_units(n, j, b) + hp + 1)
                for h in range(2):
                    mm = pe.matmul(s_ps[hp][:, h, off:CH], kT[dn % 2][0:KC, 2 * hp + h, b * P:(b + 1) * P],
                                   qT[dn % 2][0:KC, j, 2 * hp + h, off:CH], start=True, stop=True)
                mm.then_inc(s_done, 1)

            def products(i, dn, j, b, half):
                n = 2 * i + dn
                off = max(0, b - T * j) * P
                if half == 0 and b == 0:
                    pe.wait_ge(o_read, step_no(n, j))
                    if j == 0:
                        pe.wait_ge(v_ready, n + 1)
                if half == 0 and b < T * j:
                    pe.wait_ge(exp_done, FREE_S + exp_units(n, j, b + 1))
                elif half == 0:
                    pe.wait_ge(diag_done, T * step_no(n, j) + b - T * j + 1)
                cut = CH if b == 0 else max(off, CH // 2)
                start, end = (off, cut) if half == 0 else (cut, CH)
                if start < end:
                    for h in range(G):
                        mm = pe.matmul(o_ps[VW * h:VW * (h + 1), start:end], v_w[dn % 2][:, b, h, :],
                                       probs[:, b % PBUF, h, start:end], start=(b == 0), stop=(b == T * j + T - 1))
                    if end == CH:
                        mm.then_inc(pv_done, 1)

            def body(i, dn, j, final):
                last = T * j + T
                for b in range(last):
                    x = key_blocks(0, j, b)
                    aheads = (0, 1) if exists(i, dn + 1) else (0,)
                    units = [(ahead, u) for ahead in aheads for u in unit_slots.get(x - SLOTS * ahead, [])]
                    turns = [(ahead, m) for ahead, m in due(turn_slots, x) if ahead in aheads]

                    def some(quarter):
                        for ahead, u in units[len(units) * quarter // 4:len(units) * (quarter + 1) // 4]:
                            find(i, dn + ahead, u)

                    some(0)
                    scores(i, dn, j, b, 0)
                    some(1)
                    scores(i, dn, j, b, 1)
                    some(2)
                    for ahead, m in turns:
                        turn_max(i, dn + ahead, m)
                    for half in range(2):
                        if b >= 2:
                            products(i, dn, j, b - 2, half)
                        elif (dn, j) != (0, 0):
                            pdn, pj = preceding(dn, j)
                            products(i, pdn, pj, T * pj + T - 2 + b, half)
                        if half == 0:
                            some(3)
                    if b == SUM and (dn, j) != (0, 0):
                        turn_sum(i, *preceding(dn, j))
                if final:
                    for b in (last - 2, last - 1):
                        for half in range(2):
                            products(i, dn, j, b, half)
                    turn_sum(i, dn, j, True)

            pe.wait_ge(const_ok, 2)
            pe.wait_ge(ones_ok, 6)
            for x in range(MAX_FROM, 0):
                for u in unit_slots[x]:
                    find(0, 0, u)
                if x in turn_slots:
                    turn_max(0, 0, turn_slots[x])
            steps(pe, body)


def build(nc, x, w, out):
    x1 = nc.dram_tensor("x1", (TOK, E), F32, kind="Internal").ap()
    v = nc.dram_tensor("v_tok", (TOK, E), F32, kind="Internal").ap()
    qkT = nc.dram_tensor("qkT_parts", (3, 2 * E, TOK), BF16, kind="Internal").ap()
    attn = nc.dram_tensor("attn_tok", (TOK, E), F32, kind="Internal").ap()
    x2 = nc.dram_tensor("x2_tok", (TOK, E), F32, kind="Internal").ap()
    with ExitStack() as ctx:
        shared = [ctx.enter_context(nc.sbuf_tensor(name, shape, F32R)) for name, shape in
                  (("up_hi", [P, EC, F]), ("up_lo", [P, EC, F]), ("down_hi", [P, FC, E]), ("down_lo", [P, FC, E]))]
        ffn_phase(nc, True, x, x1, w, {"v": v, "qkT": qkT}, shared)
        attention_phase(nc, w, {"v": v, "qkT": qkT, "attn": attn})
        ffn_phase(nc, False, x1, out, w, {"attn": attn, "x2": x2}, shared)


def kernel(L0_attn_x, L0_attn_Wq, L0_attn_Wk, L0_attn_Wv, L0_attn_bv, L0_attn_Wo, L0_attn_bo, L0_ffn_W_fc,
           L0_ffn_W_proj):
    import numpy as np
    import concourse.bacc as bacc
    from concourse.bass_utils import run_bass_kernel_spmd

    f32 = np.float32
    inv = (f32(1.0) / f32(10000.0) ** (np.arange(0, D, 2, dtype=f32) / f32(D))).astype(f32)
    angle = np.arange(S, dtype=f32)[:, None] * inv[None, :]
    scale = f32(D ** -0.5)

    def table(t):
        return np.tile(np.concatenate([t * scale, t], axis=1).astype(f32), (B, 1))

    arrays = {
        "x": np.asarray(L0_attn_x).reshape(TOK, E),
        "up": np.asarray(L0_ffn_W_fc).T,
        "down": np.asarray(L0_ffn_W_proj).T,
        "qkv": np.concatenate([np.asarray(L0_attn_Wq).T, np.asarray(L0_attn_Wk).T, np.asarray(L0_attn_Wv).T], axis=1),
        "o": np.asarray(L0_attn_Wo).T,
        "bv": np.asarray(L0_attn_bv),
        "bo": np.asarray(L0_attn_bo),
        "cos": table(np.cos(angle)),
        "sin": table(np.sin(angle)),
        "ident": np.eye(P, dtype=f32),
        "mask": np.triu(np.full((P, P), NEG, dtype=f32), k=1),
    }
    arrays = {k: np.ascontiguousarray(a) for k, a in arrays.items()}
    nc = bacc.Bacc("TRN2", target_bir_lowering=False, num_devices=1)
    w = {k: nc.dram_tensor(f"in_{k}", a.shape, F32, kind="ExternalInput").ap() for k, a in arrays.items()}
    out = nc.dram_tensor("out", (TOK, E), F32, kind="ExternalOutput").ap()
    build(nc, w["x"], w, out)
    r = run_bass_kernel_spmd(nc, [{f"in_{k}": a for k, a in arrays.items()}], core_ids=[0])
    return r.results[0]["out"].reshape(B, S, E)
```

```python
import concourse.bass as bass
from concourse import mybir
from contextlib import ExitStack

F32 = mybir.dt.float32
F32R = mybir.dt.float32r
BF16 = mybir.dt.bfloat16
ALU = mybir.AluOpType
ACT = mybir.ActivationFunctionType
AX = mybir.AxisListType

P = 128
E = 256
EC = E // P
F = 1024
FC = F // P
B = 2
S = 2048
TOK = B * S
CH = 512
T = CH // P
NC = TOK // CH
H = 16
D = 16
G = 4
NG = H // G
EPS = 1e-5
BETA = 0.9
THRESHOLD = 1.0
STEPS = 5
HB = 4
LAG = 3
QS, KS = (0, 0, 1, 1, 0, 2), (0, 1, 0, 1, 2, 0)
NT = len(QS)
KR = NT * D
KC = KR + 3
NEG = -3.0e38


def ffn_phase(nc, first, src, dst, w, io, shared):
    tag = "a" if first else "c"
    with ExitStack() as ctx:
        def sb(name, shape, dt=F32):
            return ctx.enter_context(nc.sbuf_tensor(f"{name}_{tag}", shape, dt))

        def pb(name, shape, dt=F32):
            return ctx.enter_context(nc.psum_tensor(f"{name}_{tag}", shape, dt))

        def sem(name):
            return ctx.enter_context(nc.semaphore(f"{name}_{tag}"))

        PN = 3 * E if first else E
        up_hi, up_lo, down_hi, down_lo = shared
        proj_hi, proj_lo = sb("proj_hi", [P, EC, PN], F32R), sb("proj_lo", [P, EC, PN], F32R)
        ident, identb = sb("ident", [P, P]), sb("identb", [P, P], BF16)

        xin = sb("xin", [P, T, E])
        xn = sb("xn", [P, T, E])
        xT_hi, xT_lo = sb("xT_hi", [P, EC, CH], F32R), sb("xT_lo", [P, EC, CH], F32R)
        mT_hi, mT_lo = sb("mT_hi", [P, EC, CH], F32R), sb("mT_lo", [P, EC, CH], F32R)
        stats, mv, ln = sb("stats", [P, T, 6]), sb("mv", [P, T, 2]), sb("ln", [P, 6, T])
        relu, hsq = sb("relu", [P, 2, CH]), sb("hsq", [P, 2, CH])
        h_hi, h_lo = sb("h_hi", [P, HB, CH], F32R), sb("h_lo", [P, HB, CH], F32R)
        y = sb("y", [P, EC, CH])
        mem, part = sb("mem", [P, 2, EC, CH]), sb("part", [P, EC, CH])
        count = sb("count", [P, EC, CH], BF16)
        xres = sb("xres", [P, T, E])
        xsum = sb("xsum", [P, T, E])
        if first:
            xm = sb("xm", [P, T, E])
            mstats, mmv, mln = sb("mstats", [P, T, 6]), sb("mmv", [P, T, 2]), sb("mln", [P, 6, T])
            qk, rq, rest = (sb(n, [P, T, 2 * E]) for n in ("qk", "rq", "rest"))
            prod = sb("prod", [P, 4, E])
            parts = sb("parts", [P, T, 3, 2 * E], BF16)
            qkT = sb("qkT", [P, 12, CH], BF16)
            v = sb("v", [P, T, E])
            cosb, sinb = sb("cosb", [P, TOK // P, 2, D // 2]), sb("sinb", [P, TOK // P, 2, D // 2])
            staged = [rest[:, :, :].rearrange("p t n -> p (t n)"), qk[:, :, :].rearrange("p t n -> p (t n)"),
                      rq[:, 0:3, :].rearrange("p t n -> p (t n)")]
            split = list(zip(("up", "down", "qkv"), staged, (up_hi, down_hi, proj_hi), (up_lo, down_lo, proj_lo)))
        else:
            ain = sb("ain", [P, T, E])
            xb, x2, bias = sb("xb", [P, T, E]), sb("x2", [P, T, E]), sb("bias", [P, E])
            split = [("o", sb("stage_o", [P, EC * E])[:, :], proj_hi, proj_lo)]

        tps, yps = pb("tps", [P, EC, CH]), pb("yps", [P, EC, CH])
        ups, gps = pb("ups", [P, 2, CH]), pb("gps", [P, 2, CH])
        gpsb = [gps[:, g, :].bitcast(BF16) for g in range(2)]
        counts = tps[:, 0, :].bitcast(BF16)

        norm_steps = ("stats", "aggr", "var", "std", "rec", "sq", "err", "fix", "rstd", "norm", "T", "hi", "evac")
        names = ["w_in_" + n for n, _, _, _ in split]
        names += ["const_in", "w_hi", "w_lo", "identb_ok", "x_in", "res_in", "up_done", "relu_done", "hi_done",
                  "sq_done", "lo_done", "down_done", "y_evac", "spike", "count_T", "sum_done", "sum_out"]
        names += ["pre_" + n for n in norm_steps]
        if first:
            names += ["mid_" + n for n in norm_steps]
            names += ["qk_done", "qk_evac", "v_done", "v_evac", "v_out", "rope_mul", "rope_done",
                      "p0_done", "p1_done", "rest_done", "p2_done", "fill_done", "fill_evac", "qkT_out0", "qkT_out1"]
        else:
            names += ["a_in", "a_T", "a_hi", "a_evac", "o_done", "xb_done", "x2_done", "x2_out"]
        s = {n: sem(n) for n in names}
        passed, passed_dve, passed_sp, passed_act = (sem("passed" + x) for x in ("", "_dve", "_sp", "_act"))
        CONSTS = 16 * (3 if first else 2)
        SP = 3 * (STEPS - 1) + 1
        FROM = {"qkv": 2, "rope": 3, "p0": 5, "rest": 6, "p1": 7, "fill": 8}
        SPIKES = dict(zip([(LAG + x) % FC for x in range(FC)], (1, 1, 1, 3, 2, 2, 1, 2) if first else (1, 2, 2, 1, 2, 2, 2, 1)))
        FILLS = 2 * T
        FB = 12 // 2

        def rows(ap, c):
            return ap[bass.ds(c * CH, CH), :].rearrange("(t p) e -> p t e", p=P)

        def wait(eng, name, value):
            if not isinstance(value, int) or value > 0:
                eng.wait_ge(s[name], value)

        def turn_of(what, f):
            return (3 if f >= FROM[what] else 4), (f - FROM[what]) % FC

        def pipeline(eng, body):
            lo, hi, end = (5, NC - 1, NC + 5) if first else (3, NC - 2, NC + 3)
            for n in range(lo):
                body(n, lambda k: 0 <= n - k < NC)
            with eng.Fori(lo, hi) as it:
                body(it, lambda k: True)
            for n in range(hi, end):
                body(n, lambda k: 0 <= n - k < NC)

        block = ctx.enter_context(nc.Block())

        @block.sync
        def _(sp):
            def load_weight(i):
                name, st, _, _ = split[i]
                sp.dma_start(st.rearrange("p (c n) -> p c n", n=w[name].shape[1]),
                             w[name].rearrange("(c p) n -> p c n", p=P)).then_inc(s["w_in_" + name], 16)

            if first:
                sp.dma_start(xin[:, :, :], rows(src, 0)).then_inc(s["x_in"], 16)
                load_weight(0)
            else:
                sp.dma_start(ain[:, :, :], rows(io["attn"], 0)).then_inc(s["a_in"], 16)
                load_weight(0)
                sp.dma_start(xin[:, :, :], rows(src, 0)).then_inc(s["x_in"], 16)
            sp.dma_start(ident[:, :], w["ident"]).then_inc(s["const_in"], 16)
            if not first:
                sp.dma_start(bias[:, :], w["bo"].partition_broadcast(P)).then_inc(s["const_in"], 16)
            if first:
                for tab, name in ((cosb, "cos"), (sinb, "sin")):
                    sp.dma_start(tab[:, :, :, :], w[name].rearrange("(t p) (k i) -> p t k i", p=P, k=2))\
                      .then_inc(s["const_in"], 16)
                load_weight(1)
                load_weight(2)

            def hold(name, value):
                if not isinstance(value, int) or value > 0:
                    sp.wait_ge(s[name], value)
                    if not isinstance(value, int):
                        sp.sem_inc(passed_sp, 1)

            def load_chunk(c):
                if first:
                    hold("pre_norm", c)
                else:
                    hold("a_T", c)
                    sp.dma_start(ain[:, :, :], rows(io["attn"], c)).then_inc(s["a_in"], 16)
                    hold("xb_done", c)
                sp.dma_start(xin[:, :, :], rows(src, c)).then_inc(s["x_in"], 16)

            def body(it, has):
                if has(-1 if first else -2):
                    load_chunk(it + (1 if first else 2))
                if has(2):
                    hold("sum_done", it - 2)
                    if not first:
                        hold("x2_out", 16 * (it - 1))
                    sp.dma_start(xres[:, :, :], rows(src if first else io["x2"], it - 2)).then_inc(s["res_in"], 16)
                if first and has(4):
                    hold("v_evac", T * (it - 3))
                    sp.dma_start(rows(io["v"], it - 4), v[:, :, :]).then_inc(s["v_out"], 16)
                if not first and has(-1):
                    hold("x2_done", it + 2)
                    sp.dma_start(rows(io["x2"], it + 1), x2[:, :, :]).then_inc(s["x2_out"], 16)
                if has(2):
                    hold("sum_done", it - 1)
                    sp.dma_start(rows(dst, it - 2), xsum[:, :, :]).then_inc(s["sum_out"], 16)

            if not first:
                load_chunk(1)
                wait(sp, "x2_done", 1)
                sp.dma_start(rows(io["x2"], 0), x2[:, :, :]).then_inc(s["x2_out"], 16)
            pipeline(sp, body)
            wait(sp, "sum_out", 16 * NC)
            if first:
                wait(sp, "v_out", 16 * NC)
                wait(sp, "qkT_out0", 48 * NC)
                wait(sp, "qkT_out1", 48 * NC)
            else:
                wait(sp, "x2_out", 16 * NC)

        @block.scalar
        def _(act):
            def std(which, c, l):
                wait(act, which + "_var", c + 1)
                act.activation(l[:, 1, :], l[:, 0, :], ACT.Sqrt).then_inc(s[which + "_std"], 1)

            def high(which, c, hi, bank=tps):
                wait(act, which + "_T", c + 1)
                act.activation(hi[:, :, :], bank[:, :, :], ACT.Copy).then_inc(s[which + "_hi"], 1)

            def fill_evac(c, i):
                t, half = divmod(i, 2)
                wait(act, "fill_done", FILLS * c + i + 1)
                if i in (0, T):
                    wait(act, f"qkT_out{i // T}", 48 * c)
                act.activation(qkT[:, FB * half:FB * (half + 1), t * P:(t + 1) * P],
                               gpsb[1][:, 0:FB * P].rearrange("p (k n) -> p k n", k=FB), ACT.Copy)\
                    .then_inc(s["fill_evac"], 1)

            def v_evac(c, t):
                wait(act, "v_done", T * c + t + 1)
                wait(act, "v_out", 16 * c)
                act.activation(v[:, t, :], gps[:, 0, 0:E], ACT.Copy).then_inc(s["v_evac"], 1)

            def store_parts(c, half):
                wait(act, "fill_evac", FILLS * c + T * (half + 1))
                act.sem_inc(passed_act, 1)
                n = CH // 2
                for a in range(3):
                    act.dma_start(io["qkT"][a].rearrange("(k p) n -> p k n", p=P)[:, :, bass.ds(c * CH + half * n, n)],
                                  qkT[:, 4 * a:4 * a + 4, half * n:(half + 1) * n]).then_inc(s[f"qkT_out{half}"], 16)

            def part(c, t, k):
                if k == 0:
                    wait(act, "rope_done", 2 * (T * c + t + 1))
                    wait(act, "fill_done", FILLS * (c - 1) + 2 * t + 2)
                    act.activation(parts[:, t, 0, :], rq[:, t, :], ACT.Copy).then_inc(s["p0_done"], 1)
                else:
                    wait(act, "rest_done", T * c + t + 1)
                    act.activation(parts[:, t, 1, :], rest[:, t, :], ACT.Copy).then_inc(s["p1_done"], 1)

            def body(it, has):
                for f in range(FC):
                    if f == LAG and has(1):
                        wait(act, "down_done", FC * it)
                        wait(act, "spike", SP * (it - 1))
                        act.activation(y[:, :, :], yps[:, :, :], ACT.Copy).then_inc(s["y_evac"], 1)
                    n = it * FC + f
                    if has(0):
                        wait(act, "up_done", n + 1)
                        wait(act, "sq_done", n - 1)
                        act.activation(relu[:, f % 2, :], ups[:, f % 2, :], ACT.Relu).then_inc(s["relu_done"], 1)
                    if has(-1) and f == 7:
                        wait(act, "up_done", FC * it + FC)
                        high("pre", it + 1, xT_hi)
                    if has(0):
                        wait(act, "relu_done", n + 1)
                        wait(act, "down_done", n - HB + 1)
                        act.activation(h_hi[:, f % HB, :], relu[:, f % 2, :], ACT.Square).then_inc(s["hi_done"], 1)
                    if first and has(2) and f == 5:
                        std("mid", it - 2, mln)
                    if has(-1) and f == (2 if first else 3):
                        std("pre", it + 1, ln)
                    if not first and has(-2) and f == 5:
                        wait(act, "o_done", it + 2)
                        high("a", it + 2, mT_hi, gps)
                    if first:
                        for which, what in enumerate(("p0", "p1")):
                            k, i = turn_of(what, f)
                            if f % 2 == 1 and has(k):
                                part(it - k, i // 2, which)
                        k, i = turn_of("qkv", f)
                        if f % 2 == 1 and has(k):
                            if i < FC - 1:
                                v_evac(it - k, i // 2)
                        elif has(k):
                            c, t = it - k, i // 2
                            wait(act, "qk_done", T * c + t + 1)
                            wait(act, "rope_done", 2 * (T * (c - 1) + t + 1))
                            act.activation(qk[:, t, :], gps[:, 0, :], ACT.Copy).then_inc(s["qk_evac"], 1)
                        k, i = turn_of("fill", f)
                        if has(k):
                            fill_evac(it - k, i)
                            if i % T == T - 1:
                                store_parts(it - k, i // T)
                        if f == 0 and has(4):
                            v_evac(it - 4, T - 1)
                        if f == 0 and has(3):
                            wait(act, "v_done", T * (it - 3))
                            high("mid", it - 3, mT_hi)

            for name, st, hi, _ in split:
                act.wait_ge(s["w_in_" + name], 16)
                act.activation(hi[:, :, :].rearrange("p c n -> p (c n)"), st, ACT.Copy).then_inc(s["w_hi"], 1)
                if name in ("up", "o"):
                    act.wait_ge(s["const_in"], CONSTS)
                    act.activation(identb[:, :], ident[:, :], ACT.Copy).then_inc(s["identb_ok"], 1)
                    if not first:
                        high("a", 0, mT_hi, gps)
                        std("pre", 0, ln)
                        act.wait_ge(s["o_done"], 1)
                        high("a", 1, mT_hi, gps)
                    else:
                        std("pre", 0, ln)
                    high("pre", 0, xT_hi)
            pipeline(act, body)

        @block.vector
        def _(dve):
            def norm_stats(which, c, x, st, m, l):
                for t in range(T):
                    dve.bn_stats(st[:, t, :], x[:, t, :]).then_inc(s[which + "_stats"], 1)
                wait(dve, which + "_stats", T * c + T)
                dve.sem_inc(passed_dve, 1)
                for t in range(T):
                    dve.bn_aggr(m[:, t, :], st[:, t, :]).then_inc(s[which + "_aggr"], 1)
                wait(dve, which + "_aggr", T * c + T)
                dve.tensor_scalar(l[:, 0, :], m[:, :, 1], EPS, None, ALU.add).then_inc(s[which + "_var"], 1)

            def norm(which, c, x, o, m, l):
                wait(dve, which + "_std", c + 1)
                dve.reciprocal(l[:, 2, :], l[:, 1, :]).then_inc(s[which + "_rec"], 1)
                wait(dve, which + "_rec", c + 1)
                dve.tensor_tensor(l[:, 3, :], l[:, 2, :], l[:, 2, :], ALU.mult).then_inc(s[which + "_sq"], 1)
                wait(dve, which + "_sq", c + 1)
                dve.tensor_tensor(l[:, 4, :], l[:, 3, :], l[:, 0, :], ALU.mult).then_inc(s[which + "_err"], 1)
                wait(dve, which + "_err", c + 1)
                dve.tensor_scalar(l[:, 5, :], l[:, 4, :], -0.5, 1.5, ALU.mult, ALU.add).then_inc(s[which + "_fix"], 1)
                wait(dve, which + "_fix", c + 1)
                dve.tensor_tensor(l[:, 3, :], l[:, 2, :], l[:, 5, :], ALU.mult).then_inc(s[which + "_rstd"], 1)
                wait(dve, which + "_rstd", c + 1)
                wait(dve, which + "_T", c)
                for t in range(T):
                    last = dve.tensor_scalar(o[:, t, :], x[:, t, :], m[:, t, 0:1], l[:, 3, t:t + 1],
                                             ALU.subtract, ALU.mult)
                last.then_inc(s[which + "_norm"], 1)

            def low(which, c, hi, lo, bank=tps):
                wait(dve, which + "_hi", c + 1)
                dve.tensor_tensor(lo[:, :, :], bank[:, :, :], hi[:, :, :].bitcast(F32), ALU.subtract)\
                   .then_inc(s[which + "_evac"], 1)

            def spikes(c, k0, k1):
                for k in range(k0, k1):
                    step, what = (k - 1) // 3, (k - 1) % 3
                    cur, sign, above = (y, 1.0, ALU.is_gt) if step == 0 else (mem[:, (step - 1) % 2], -1.0, ALU.is_lt)
                    cur = cur[:, :, :] if step == 0 else cur
                    if k == 0:
                        wait(dve, "y_evac", c + 1)
                        wait(dve, "count_T", c)
                        dve.tensor_scalar(count[:, :, :], y[:, :, :], THRESHOLD, None, ALU.is_gt)\
                           .then_inc(s["spike"], 1)
                        continue
                    wait(dve, "spike", SP * c + k)
                    if what == 0:
                        dve.scalar_tensor_tensor(out=part[:, :, :], in0=cur, scalar=sign * BETA, in1=y[:, :, :],
                                                 op0=ALU.mult, op1=ALU.add).then_inc(s["spike"], 1)
                    elif what == 1:
                        dve.scalar_tensor_tensor(out=mem[:, step % 2], in0=cur, scalar=sign * THRESHOLD,
                                                 in1=part[:, :, :], op0=above, op1=ALU.subtract)\
                           .then_inc(s["spike"], 1)
                    else:
                        dve.scalar_tensor_tensor(out=count[:, :, :], in0=mem[:, step % 2], scalar=-THRESHOLD,
                                                 in1=count[:, :, :], op0=ALU.is_lt, op1=ALU.add)\
                           .then_inc(s["spike"], 1)

            def sum_(c):
                wait(dve, "count_T", c + 1)
                wait(dve, "res_in", 16 * (c + 1))
                wait(dve, "sum_out", 16 * c)
                dve.scalar_tensor_tensor(out=xsum[:, :, :].rearrange("p t e -> p (t e)"), in0=counts,
                                         scalar=0.5 / STEPS, in1=xres[:, :, :].rearrange("p t e -> p (t e)"),
                                         op0=ALU.mult, op1=ALU.add).then_inc(s["sum_done"], 1)

            def attn_sum(c):
                wait(dve, "o_done", c + 1)
                wait(dve, "xb_done", c + 1)
                wait(dve, "x2_out", 16 * c)
                dve.tensor_tensor(x2[:, :, :].rearrange("p t e -> p (t e)"), gps[:, :, :].rearrange("p g n -> p (g n)"),
                                  xb[:, :, :].rearrange("p t e -> p (t e)"), ALU.add).then_inc(s["x2_done"], 1)
                wait(dve, "x2_done", c + 1)

            def body(it, has):
                for f in range(FC):
                    if first and f == 1 and has(3):
                        low("mid", it - 3, mT_hi, mT_lo)
                    if not first and f == 1 and has(-1):
                        attn_sum(it + 1)
                    if f == 7 and has(-1):
                        low("pre", it + 1, xT_hi, xT_lo)
                    k = 1 if f >= LAG else 2
                    if f != LAG and has(k):
                        before = sum(SPIKES[x % FC] for x in range(LAG, f + FC * (f < LAG)))
                        spikes(it - k, before, before + SPIKES[f])
                    if has(0):
                        n = it * FC + f
                        wait(dve, "sq_done", n + 1)
                        wait(dve, "hi_done", n + 1)
                        wait(dve, "down_done", n - HB + 1)
                        dve.tensor_tensor(h_lo[:, f % HB, :], hsq[:, f % 2, :], h_hi[:, f % HB, :].bitcast(F32),
                                          ALU.subtract).then_inc(s["lo_done"], 1)
                    if not first and f == 6 and has(-2):
                        low("a", it + 2, mT_hi, mT_lo, gps)
                    if f == LAG and has(k):
                        spikes(it - k, 0, SPIKES[f])
                    if f == 3 and has(2):
                        sum_(it - 2)
                    if f == (0 if first else 2) and has(-1):
                        if first:
                            wait(dve, "x_in", 16 * (it + 2))
                        norm_stats("pre", it + 1, xin if first else x2, stats, mv, ln)
                    if f == (3 if first else 4) and has(-1):
                        norm("pre", it + 1, xin if first else x2, xn, mv, ln)
                    if first and f == 4 and has(2):
                        wait(dve, "sum_done", it - 1)
                        norm_stats("mid", it - 2, xsum, mstats, mmv, mln)
                    if first and f == 6 and has(2):
                        norm("mid", it - 2, xsum, xm, mmv, mln)
                    if first and f % 2 == 1:
                        q, i = turn_of("p1", f)
                        if has(q):
                            c, t = it - q, i // 2
                            wait(dve, "p1_done", T * c + t + 1)
                            dve.tensor_tensor(parts[:, t, 2, :], rest[:, t, :], parts[:, t, 1, :], ALU.subtract)\
                               .then_inc(s["p2_done"], 1)

            def split_low(i):
                _, st, hi, lo = split[i]
                dve.wait_ge(s["w_hi"], i + 1)
                dve.tensor_tensor(lo[:, :, :].rearrange("p c n -> p (c n)"), st,
                                  hi[:, :, :].rearrange("p c n -> p (c n)").bitcast(F32), ALU.subtract)\
                   .then_inc(s["w_lo"], 1)

            if first:
                wait(dve, "x_in", 16)
                norm_stats("pre", 0, xin, stats, mv, ln)
                split_low(0)
                norm("pre", 0, xin, xn, mv, ln)
            else:
                split_low(0)
                low("a", 0, mT_hi, mT_lo, gps)
                attn_sum(0)
                norm_stats("pre", 0, x2, stats, mv, ln)
                norm("pre", 0, x2, xn, mv, ln)
                low("a", 1, mT_hi, mT_lo, gps)
            low("pre", 0, xT_hi, xT_lo)
            if first:
                split_low(1)
                split_low(2)
            pipeline(dve, body)

        @block.gpsimd
        def _(pool):
            def rope(c, t, half):
                n = 2 * (T * c + t) + half
                if half == 0:
                    wait(pool, "qk_evac", T * c + t + 1)
                x = qk[:, t, :].rearrange("p (k h i two) -> p k h i two", k=2, h=H, two=2)
                o = rq[:, t, :].rearrange("p (h i two) -> p h i two", i=D // 2, two=2)

                def table(tab):
                    return tab[:, bass.ds(T * c + t, 1), :, :].rearrange("p o k i -> p (o k) i").unsqueeze(2)\
                        .broadcast_to([P, 2, H, D // 2])

                wait(pool, "rope_done", n - 1)
                pool.sem_inc(passed, 1)
                for m, tab in enumerate((sinb, cosb) if half else (cosb, sinb)):
                    pool.tensor_tensor(prod[:, 2 * half + m, :].rearrange("p (k h i) -> p k h i", k=2, h=H),
                                       x[:, :, :, :, m], table(tab), ALU.mult).then_inc(s["rope_mul"], 1)
                wait(pool, "rope_mul", 2 * n + 2)
                wait(pool, "rest_done", T * (c - 1) + t + 1)
                p4 = prod[:, :, :].rearrange("p n (h i) -> p n h i", i=D // 2)
                pool.tensor_tensor(o[:, :, :, half], p4[:, 2 * half], p4[:, 2 * half + 1],
                                   ALU.add if half else ALU.subtract).then_inc(s["rope_done"], 1)

            def add_bias(c):
                wait(pool, "x_in", 16 * (c + 1))
                wait(pool, "x2_done", c)
                pool.tensor_tensor(xb[:, :, :], xin[:, :, :], bias[:, :].unsqueeze(1).broadcast_to([P, T, E]), ALU.add)\
                    .then_inc(s["xb_done"], 1)

            def body(it, has):
                for f in range(FC):
                    if has(0):
                        n = it * FC + f
                        wait(pool, "relu_done", n + 1)
                        wait(pool, "lo_done", n - 1)
                        pool.tensor_tensor(hsq[:, f % 2, :], relu[:, f % 2, :], relu[:, f % 2, :], ALU.mult)\
                            .then_inc(s["sq_done"], 1)
                    if first:
                        k, i = turn_of("rope", f)
                        if has(k):
                            rope(it - k, i // 2, i % 2)
                        k, i = turn_of("rest", f)
                        if f % 2 == 0 and has(k):
                            c, t = it - k, i // 2
                            wait(pool, "p0_done", T * c + t + 1)
                            wait(pool, "p2_done", T * (c - 1) + t + 1)
                            pool.tensor_tensor(rest[:, t, :], rq[:, t, :], parts[:, t, 0, :], ALU.subtract)\
                                .then_inc(s["rest_done"], 1)
                    if not first and has(-2) and f == 4:
                        add_bias(it + 2)

            wait(pool, "const_in", CONSTS)
            if first:
                wait(pool, "w_lo", 3)
            else:
                add_bias(0)
                add_bias(1)
            pipeline(pool, body)

        @block.tensor
        def _(pe):
            def up(it, f):
                n = it * FC + f
                if f == 0:
                    wait(pe, "pre_evac", it + 1)
                wait(pe, "relu_done", n - 1)
                for i, (wt, x, c) in enumerate([(a, b, c) for c in range(EC) for a, b in
                                                ((up_hi, xT_hi), (up_hi, xT_lo), (up_lo, xT_hi))]):
                    last = pe.matmul(ups[:, f % 2, :], wt[:, c, f * P:(f + 1) * P], x[:, c, :],
                                     start=(i == 0), stop=(i == 3 * EC - 1))
                last.then_inc(s["up_done"], 1)

            def down(it, f):
                if f == 0:
                    wait(pe, "y_evac", it)
                    if first and isinstance(it, int) and it == 0:
                        wait(pe, "w_lo", 2)
                wait(pe, "lo_done", it * FC + f + 1)
                for c in range(EC):
                    for i, (wt, h) in enumerate(((down_hi, h_hi), (down_hi, h_lo), (down_lo, h_hi))):
                        last = pe.matmul(yps[:, c, :], wt[:, f, c * P:(c + 1) * P], h[:, f % HB, :],
                                         start=(f == 0 and i == 0), stop=(f == FC - 1 and i == 2))
                last.then_inc(s["down_done"], 1)

            def turn(x, done, bank=tps):
                for t in range(T):
                    for c in range(EC):
                        last = pe.transpose(bank[:, c, t * P:(t + 1) * P], x[:, t, c * P:(c + 1) * P], ident[:, :])
                last.then_inc(s[done], 1)

            def count_turn(c):
                wait(pe, "spike", SP * (c + 1))
                for t in range(T):
                    for k in range(EC):
                        last = pe.transpose(counts[:, t * E + k * P:t * E + (k + 1) * P],
                                            count[:, k, t * P:(t + 1) * P], identb[:, :])
                last.then_inc(s["count_T"], 1)

            def fill(c, i):
                t, half = divmod(i, 2)
                if half == 0:
                    wait(pe, "p2_done", T * c + t + 1)
                wait(pe, "fill_evac", FILLS * c + i)
                for b in range(FB):
                    a, blk = divmod(FB * half + b, 4)
                    last = pe.transpose(gpsb[1][:, b * P:(b + 1) * P], parts[:, t, a, blk * P:(blk + 1) * P],
                                        identb[:, :])
                last.then_inc(s["fill_done"], 1)

            def project(out, t, c0, c1):
                for i, (wt, x, c) in enumerate([(a, b, c) for c in range(EC) for a, b in
                                                ((proj_hi, mT_hi), (proj_hi, mT_lo), (proj_lo, mT_hi))]):
                    last = pe.matmul(out, x[:, c, t * P:(t + 1) * P], wt[:, c, c0:c1],
                                     start=(i == 0), stop=(i == 3 * EC - 1))
                return last

            def qkv(c, i):
                t = i // 2
                if i == 0:
                    wait(pe, "mid_evac", c + 1)
                if i % 2 == 0:
                    wait(pe, "v_evac", T * c + t)
                    project(gps[:, 0, :], t, 0, 2 * E).then_inc(s["qk_done"], 1)
                else:
                    wait(pe, "qk_evac", T * c + t + 1)
                    project(gps[:, 0, 0:E], t, 2 * E, 3 * E).then_inc(s["v_done"], 1)

            def attn_turn(c):
                wait(pe, "a_in", 16 * (c + 1))
                wait(pe, "x2_done", c)
                turn(ain, "a_T", gps)

            def attn_out(c):
                wait(pe, "a_evac", c + 1)
                for t in range(T):
                    last = project(gps[:, t // 2, (t % 2) * E:(t % 2 + 1) * E], t, 0, E)
                last.then_inc(s["o_done"], 1)

            def body(it, has):
                for f in range(FC):
                    if f > 0 and has(0):
                        up(it, f)
                    if f == 3 and has(2):
                        if first and has(3):
                            wait(pe, "mid_evac", it - 2)
                        count_turn(it - 2)
                    if not first and f == 1 and has(-1):
                        attn_out(it + 1)
                    k = 0 if f >= LAG else 1
                    if has(k):
                        down(it - k, (f - LAG) % FC)
                    if first:
                        k, i = turn_of("qkv", f)
                        if has(k) and i < FC - 1:
                            qkv(it - k, i)
                        k, i = turn_of("fill", f)
                        if has(k):
                            fill(it - k, i)
                    if f == 6 and has(-1):
                        wait(pe, "pre_norm", it + 2)
                        if has(2):
                            wait(pe, "sum_done", it - 1)
                        turn(xn, "pre_T")
                    if f == 0 and has(0):
                        up(it, 0)
                    if first and f == 0 and has(4):
                        qkv(it - 4, FC - 1)
                    if first and f == 0 and has(3):
                        wait(pe, "mid_norm", it - 2)
                        turn(xm, "mid_T")
                    if not first and f == 5 and has(-2):
                        attn_turn(it + 2)

            wait(pe, "const_in", CONSTS)
            wait(pe, "identb_ok", 1)
            if not first:
                attn_turn(0)
                wait(pe, "w_lo", 1)
                attn_out(0)
                attn_turn(1)
            wait(pe, "pre_norm", 1)
            turn(xn, "pre_T")
            if first:
                wait(pe, "w_lo", 1)
            pipeline(pe, body)


def attention_phase(nc, w, io):
    with ExitStack() as ctx:
        def sb(name, shape, dt=F32):
            return ctx.enter_context(nc.sbuf_tensor(name, shape, dt))

        def pb(name, shape, dt=F32):
            return ctx.enter_context(nc.psum_tensor(name, shape, dt))

        def sem(name):
            return ctx.enter_context(nc.semaphore(name))

        KB = S // P
        NJ = S // CH
        PAIRS = B * NG // 2
        PBUF = 4
        VW = 32

        qT = [sb(f"qT{p}", [P, NJ, G, CH], BF16) for p in range(2)]
        kT = [sb(f"kT{p}", [P, G, S], BF16) for p in range(2)]
        v_in = [sb(f"v_in{p}", [P, KB, G * D]) for p in range(2)]
        v_w = [sb(f"v_w{p}", [P, KB, G, VW]) for p in range(2)]
        probs = sb("probs", [P, PBUF, G, CH])
        ident, identb = sb("ident_b", [P, P]), sb("identb_b", [P, P], BF16)
        bias = sb("bias_b", [P, E])
        mask, maskb = sb("mask_b", [P, P]), sb("maskb", [P, P], BF16)
        maxes = sb("maxes", [P, 2, G, T, NJ])
        negmax, negrest = sb("negmax", [P, G * T]), sb("negrest", [P, G * T])
        negparts = sb("negparts", [P, P // (G * T), G * T], BF16)
        shiftT = sb("shiftT", [3 * G * T, P], BF16)
        osum = sb("osum", [P, CH])
        denom = sb("denom", [P, T * G])
        att = sb("att", [P, T, G * D])

        s_ps = [pb(f"s_ps{p}", [P, 2, CH]) for p in range(2)]
        m_ps = pb("m_ps", [P, 2, CH])
        o_ps = pb("o_ps", [P, CH])
        t_ps = pb("t_ps", [P, CH])

        const_in, const_ok, ones_ok = sem("const_in_b"), sem("const_ok_b"), sem("ones_ok")
        qk_in = [sem(f"qk_in{p}") for p in range(2)]
        vs_in = [sem(f"vs_in{p}") for p in range(2)]
        v_ready, s_done, exp_done, diag_done, pv_done = (sem(n) for n in (
            "v_ready", "s_done", "exp_done", "diag_done", "pv_done"))
        max_done, max_read, neg_done, neg_step, neg_turned, neg_out, shift_in = (sem(n) for n in (
            "max_done", "max_read", "neg_done", "neg_step", "neg_turned", "neg_out", "shift_in"))
        neg_zero, bias_in = sem("neg_zero"), sem("bias_in")
        passed = sem("passed_b")
        o_read, o_turned, denom_done, att_done, att_out = (sem(n) for n in (
            "o_read", "o_turned", "denom_done", "att_done", "att_out"))

        def step_no(n, j):
            return NJ * n + j

        def exp_units(n, j, i):
            return 80 * n + 4 * j * (j + 1) + 2 * i

        def key_blocks(n, j, i):
            return 40 * n + 2 * j * (j + 1) + i

        SLOTS = NJ * (NJ + 1) * T // 2
        UNITS = [(j, t, h, k, CH if k < j else P * (t + 1))
                 for j in range(NJ) for t in range(T) for h in range(G) for k in range(j + 1)]
        MAX_FROM, MAX_TO = -20, 20

        def place_units():
            cost = [u[4] + 110 for u in UNITS]
            room = []
            for s in range(MAX_FROM, MAX_TO):
                j, b = [(j, b) for j in range(NJ) for b in range(T * j + T)][s % SLOTS]
                room.append(1 + T - max(0, b - T * j))
            slots, done, full, u = {}, 0, 0, 0
            for s, r in zip(range(MAX_FROM, MAX_TO), room):
                full += r * sum(cost) / sum(room)
                slots[s] = []
                while u < len(UNITS) and (done + cost[u] / 2 <= full):
                    slots[s].append(u)
                    done += cost[u]
                    u += 1
            assert u == len(UNITS)
            return slots

        unit_slots = place_units()
        NEG_OPS = 5

        def vector_items():
            items, pending = {}, []
            for s in sorted(unit_slots):
                items[s] = []
                for u in unit_slots[s]:
                    items[s].append(("unit", u))
                    if u + 1 == len(UNITS) or UNITS[u + 1][0] > UNITS[u][0]:
                        pending = [(UNITS[u][0], k) for k in range(NEG_OPS)]
                    if pending:
                        items[s].append(("negate", pending.pop(0)))
            items[s] += [("negate", x) for x in pending]
            return items

        vector_slots = vector_items()
        found = [max(s for s in vector_slots if ("negate", (m, NEG_OPS - 1)) in vector_slots[s]) for m in range(NJ)]
        SUM = 3
        sum_slots = [2 * j * (j + 1) + SUM for j in range(NJ)]
        turn_slots = {f + 1: m for m, f in enumerate(found)}
        out_slots = {x if x % SLOTS in sum_slots else x + 1: m for x, m in turn_slots.items()}

        def due(slots, s):
            return [(ahead, slots[x]) for ahead, x in ((0, s), (1, s - SLOTS)) if x in slots]

        def turns_before_sum(j):
            return sum(x <= sum_slots[j] for x in turn_slots) + sum(SLOTS + x <= sum_slots[j] for x in turn_slots)

        def sums_before_turn(m):
            x = found[m] + 1
            return sum(y < x for y in sum_slots) - sum(y >= x + SLOTS for y in sum_slots) - 1

        LOADS = 16 * NT * (NJ + 1)
        FREE_P, FREE_S, FREE_M = PBUF, 2, 2

        def wait(eng, sem, value):
            if not isinstance(value, int) or value > 0:
                eng.wait_ge(sem, value)

        def preceding(dn, j):
            return (dn, j - 1) if j else (dn - 1, NJ - 1)

        def exists(i, dn):
            return not isinstance(i, int) or 2 * i + dn < B * NG

        def steps(eng, body):
            turn = [(dn, j) for dn in range(2) for j in range(NJ)][2:] + [(2, 0), (2, 1)]
            body(0, 0, 0, False)
            body(0, 0, 1, False)
            with eng.Fori(0, PAIRS - 1) as i:
                for dn, j in turn:
                    body(i, dn, j, False)
            for dn, j in turn[:-2]:
                body(PAIRS - 1, dn, j, (dn, j) == (1, NJ - 1))

        def place(i, dn):
            i, dn = i + dn // 2, dn % 2
            return (i // 2) * S, ((i % 2) * 2 + dn) * (G * D)

        block = ctx.enter_context(nc.Block())

        @block.sync
        def _(sp):
            sp.dma_start(ident[:, :], w["ident"]).then_inc(const_in, 16)
            sp.dma_start(mask[:, :], w["mask"]).then_inc(const_in, 16)
            sp.dma_start(bias[:, :], w["bv"].partition_broadcast(P)).then_inc(bias_in, 16)

            def load(i, dn, terms):
                tok, row = place(i, dn)
                p = dn % 2
                for m in terms:
                    q, k = (io["qkT"][a, bass.ds(row + first, G * D), bass.ds(tok, S)] for a, first in
                            ((QS[m], 0), (KS[m], E)))
                    for j in range(NJ):
                        sp.dma_start(qT[p][D * m:D * (m + 1), j, :, :],
                                     q[:, j * CH:(j + 1) * CH].rearrange("(h d) t -> d h t", d=D))\
                          .then_inc(qk_in[p], 16)
                    sp.dma_start(kT[p][D * m:D * (m + 1), :, :], k.rearrange("(h d) t -> d h t", d=D))\
                      .then_inc(qk_in[p], 16)
                    if m == 0:
                        sp.dma_start(v_in[p][:, :, :], io["v"][bass.ds(tok, S), bass.ds(row, G * D)]
                                     .rearrange("(k p) n -> p k n", p=P)).then_inc(vs_in[p], 16)

            def shift(i, dn, j):
                n = 2 * i + dn
                sp.wait_ge(neg_out, step_no(n, j) + 1)
                for a in range(3):
                    sp.dma_start(qT[dn % 2][KR + a:KR + a + 1, j, :, :],
                                 shiftT[a * G * T:(a + 1) * G * T, :]).then_inc(shift_in, 16)

            def body(i, dn, j, final):
                n = 2 * i + dn
                if j < 3 and exists(i, dn + 1):
                    if j == 0 and (dn > 0):
                        sp.wait_ge(s_done, exp_units(n, 0, 0))
                        sp.wait_ge(v_ready, n)
                    load(i, dn + 1, (2 * j, 2 * j + 1))
                for b in range(T * j + T):
                    if b == SUM and (dn, j) != (0, 0):
                        store(i, *preceding(dn, j))
                    for ahead, m in due(out_slots, key_blocks(0, j, b)):
                        if exists(i, dn + ahead):
                            shift(i, dn + ahead, m)
                if final:
                    store(i, dn, j)

            def store(i, dn, j):
                tok, row = place(i, dn)
                sp.wait_ge(att_done, step_no(2 * i + dn, j) + 1)
                sp.dma_start(io["attn"][bass.ds(tok + j * CH, CH), bass.ds(row, G * D)]
                             .rearrange("(t p) n -> p t n", p=P), att[:, :, :]).then_inc(att_out, 16)

            load(0, 0, range(NT))
            for x in range(MAX_FROM, 0):
                if x in out_slots:
                    shift(0, 0, out_slots[x])
            steps(sp, body)
            sp.wait_ge(att_out, 16 * NJ * B * NG)

        @block.gpsimd
        def _(pool):
            for p in range(2):
                pool.memset(kT[p][KR:KC, :, :], 1.0).then_inc(ones_ok, 1)
                pool.wait_ge(ones_ok, 3 * p + 1)
                pool.memset(v_w[p][:, :, :, :], 0.0).then_inc(ones_ok, 1)
                pool.wait_ge(ones_ok, 3 * p + 2)
                pool.memset(v_w[p][:, :, :, D:D + 1], 1.0).then_inc(ones_ok, 1)
                pool.wait_ge(ones_ok, 3 * p + 3)

            def widen(i, dn):
                _, row = place(i, dn)
                pool.wait_ge(vs_in[dn % 2], 16 * (i + dn // 2 + 1))
                pool.sem_inc(passed, 1)
                pool.tensor_tensor(v_w[dn % 2][:, :, :, 0:D],
                                   v_in[dn % 2][:, :, :].rearrange("p k (h d) -> p k h d", d=D),
                                   bias[:, bass.ds(row, G * D)].rearrange("p (h d) -> p h d", d=D).unsqueeze(1)
                                   .broadcast_to([P, KB, G, D]), ALU.add).then_inc(v_ready, 1)

            pool.wait_ge(bias_in, 16)
            widen(0, 0)

            def body(i, dn, j, final):
                n = 2 * i + dn
                for a in range(T):
                    pool.wait_ge(exp_done, FREE_S + exp_units(n, j, T * j + a + 1))
                    tile = probs[:, (T * j + a) % PBUF, :, P * a:P * (a + 1)]
                    pool.sem_inc(passed, 1)
                    pool.affine_select(out=tile, in_=tile, compare_op=ALU.is_ge, fill=0.0, base=0,
                                       pattern=[[0, G], [1, P]], channel_multiplier=-1).then_inc(diag_done, 1)
                if j == 1 and exists(i, dn + 1):
                    widen(i, dn + 1)

            steps(pool, body)

        @block.scalar
        def _(act):
            act.sem_inc(exp_done, FREE_S)
            act.wait_ge(const_in, 32)
            act.activation(identb[:, :], ident[:, :], ACT.Copy).then_inc(const_ok, 1)
            act.activation(maskb[:, :], mask[:, :], ACT.Copy).then_inc(const_ok, 1)

            def read_sum(i, dn, j):
                n = 2 * i + dn
                act.wait_ge(pv_done, FREE_P + key_blocks(n, j, T * j + T))
                act.wait_ge(o_turned, step_no(n, j))
                act.activation(osum[:, :], o_ps[:, :], ACT.Copy).then_inc(o_read, 1)

            def body(i, dn, j, final):
                n = 2 * i + dn
                for b in range(T * j + T):
                    off = max(0, b - T * j) * P
                    act.wait_ge(pv_done, key_blocks(n, j, b) + 1)
                    for hp in range(2):
                        act.wait_ge(s_done, exp_units(n, j, b) + hp + 1)
                        act.activation(probs[:, b % PBUF, 2 * hp:2 * hp + 2, off:CH], s_ps[hp][:, :, off:CH], ACT.Exp)\
                           .then_inc(exp_done, 1)
                    if b == 1 and (dn, j) != (0, 0):
                        read_sum(i, *preceding(dn, j))
                if final:
                    read_sum(i, dn, j)

            steps(act, body)

        @block.vector
        def _(dve):
            dve.sem_inc(max_read, FREE_M)
            dve.memset(negparts[:, :, :], 0.0).then_inc(neg_zero, 1)
            dve.wait_ge(neg_zero, 1)

            def unit(i, dn, u):
                n = 2 * i + dn
                j, t, h, k, width = UNITS[u]
                dve.wait_ge(max_done, len(UNITS) * n + u + 1)
                dve.tensor_reduce(maxes[:, j % 2, h, t, k:k + 1], m_ps[:, u % 2, 0:width], AX.X, ALU.max)\
                   .then_inc(max_read, 1)

            def negate(i, dn, j, k):
                n = 2 * i + dn
                t = step_no(n, j)
                if k == 0:
                    dve.wait_ge(max_read, FREE_M + len(UNITS) * n + 8 * (j + 1) * (j + 2))
                    dve.tensor_reduce(negmax[:, :], maxes[:, j % 2, :, :, 0:j + 1].rearrange("p h t k -> p (h t) k"), AX.X,
                                      ALU.max, negate=True).then_inc(neg_step, 1)
                elif k == 1:
                    dve.wait_ge(neg_step, 4 * t + 1)
                    wait(dve, neg_turned, t)
                    dve.tensor_copy(negparts[:, 0, :], negmax[:, :]).then_inc(neg_step, 1)
                elif k == 2:
                    dve.wait_ge(neg_step, 4 * t + 2)
                    dve.tensor_tensor(negrest[:, :], negmax[:, :], negparts[:, 0, :], ALU.subtract).then_inc(neg_step, 1)
                elif k == 3:
                    dve.wait_ge(neg_step, 4 * t + 3)
                    dve.tensor_copy(negparts[:, 1, :], negrest[:, :]).then_inc(neg_step, 1)
                else:
                    dve.wait_ge(neg_step, 4 * t + 4)
                    dve.tensor_tensor(negparts[:, 2, :], negrest[:, :], negparts[:, 1, :], ALU.subtract)\
                       .then_inc(neg_done, 1)

            def send(i, dn, j):
                t = step_no(2 * i + dn, j)
                dve.wait_ge(neg_turned, t + 1)
                wait(dve, shift_in, 48 * t)
                dve.tensor_copy(shiftT[:, :], t_ps[:, 0:P // 2].bitcast(BF16)[0:3 * G * T, :]).then_inc(neg_out, 1)

            def normalise(i, dn, j):
                n = 2 * i + dn
                t = step_no(n, j)
                dve.wait_ge(o_turned, t + 1)
                sums = t_ps[:, :].rearrange("p (g w) -> p g w", w=VW)
                dve.reciprocal(denom[:, :].unsqueeze(2), sums[:, :, D:D + 1]).then_inc(denom_done, 1)
                dve.wait_ge(denom_done, t + 1)
                dve.wait_ge(att_out, 16 * t)
                dve.tensor_tensor(att[:, :, :].rearrange("p t (h d) -> p (t h) d", d=D), sums[:, :, 0:D],
                                  denom[:, :].unsqueeze(2).broadcast_to([P, T * G, D]), ALU.mult)\
                   .then_inc(att_done, 1)

            def slot(i, dn, x, ahead):
                for kind, what in vector_slots.get(x, []):
                    if kind == "unit":
                        unit(i, dn + ahead, what)
                    else:
                        negate(i, dn + ahead, *what)
                if x in out_slots:
                    send(i, dn + ahead, out_slots[x])

            def body(i, dn, j, final):
                for b in range(T * j + T):
                    x = key_blocks(0, j, b)
                    slot(i, dn, x, 0)
                    if exists(i, dn + 1):
                        slot(i, dn, x - SLOTS, 1)
                    if b == SUM and (dn, j) != (0, 0):
                        normalise(i, *preceding(dn, j))
                if final:
                    normalise(i, dn, j)

            for x in range(MAX_FROM, 0):
                slot(0, 0, x, 0)
            steps(dve, body)

        @block.tensor
        def _(pe):
            pe.sem_inc(pv_done, FREE_P)

            def find(i, dn, u):
                n = 2 * i + dn
                j, t, h, k, width = UNITS[u]
                if u == 0:
                    pe.wait_ge(qk_in[dn % 2], LOADS * (i + dn // 2 + 1))
                pe.wait_ge(max_read, len(UNITS) * n + u + 1)
                q = qT[dn % 2][0:KR, j, h, t * P:(t + 1) * P]
                mm = pe.matmul(m_ps[:, u % 2, 0:width], q, kT[dn % 2][0:KR, h, k * CH:k * CH + width],
                               start=True, stop=(k < j))
                if k == j:
                    mm = pe.matmul(m_ps[:, u % 2, width - P:width], identb[:, :], maskb[:, :], start=False, stop=True)
                mm.then_inc(max_done, 1)

            def turn_max(i, dn, j):
                n = 2 * i + dn
                wait(pe, att_done, NJ * n + sums_before_turn(j))
                wait(pe, neg_out, step_no(n, j))
                pe.wait_ge(neg_done, step_no(n, j) + 1)
                pe.transpose(t_ps[:, 0:P // 2].bitcast(BF16), negparts[:, :, :].rearrange("p a c -> p (a c)"),
                             identb[:, :]).then_inc(neg_turned, 1)

            def turn_sum(i, dn, j, final=False):
                n = 2 * i + dn
                wait(pe, att_done, step_no(n, j))
                turned = NJ * (n + (j + 1) // NJ) + turns_before_sum((j + 1) % NJ)
                if exists(i, dn + 1):
                    pe.wait_ge(neg_out, turned)
                else:
                    pe.wait_ge(neg_out, min(turned, NJ * B * NG))
                pe.wait_ge(o_read, step_no(n, j) + 1)
                for t in range(T):
                    mm = pe.transpose(t_ps[:, t * P:(t + 1) * P], osum[:, t * P:(t + 1) * P], ident[:, :])
                mm.then_inc(o_turned, 1)

            def scores(i, dn, j, b, hp):
                n = 2 * i + dn
                off = max(0, b - T * j) * P
                if b == 0 and hp == 0:
                    pe.wait_ge(shift_in, 48 * (step_no(n, j) + 1))
                pe.wait_ge(exp_done, exp_units(n, j, b) + hp + 1)
                for h in range(2):
                    mm = pe.matmul(s_ps[hp][:, h, off:CH], kT[dn % 2][0:KC, 2 * hp + h, b * P:(b + 1) * P],
                                   qT[dn % 2][0:KC, j, 2 * hp + h, off:CH], start=True, stop=True)
                mm.then_inc(s_done, 1)

            def products(i, dn, j, b, half):
                n = 2 * i + dn
                off = max(0, b - T * j) * P
                if half == 0 and b == 0:
                    pe.wait_ge(o_read, step_no(n, j))
                    if j == 0:
                        pe.wait_ge(v_ready, n + 1)
                if half == 0 and b < T * j:
                    pe.wait_ge(exp_done, FREE_S + exp_units(n, j, b + 1))
                elif half == 0:
                    pe.wait_ge(diag_done, T * step_no(n, j) + b - T * j + 1)
                cut = CH if b == 0 else max(off, CH // 2)
                start, end = (off, cut) if half == 0 else (cut, CH)
                if start < end:
                    for h in range(G):
                        mm = pe.matmul(o_ps[VW * h:VW * (h + 1), start:end], v_w[dn % 2][:, b, h, :],
                                       probs[:, b % PBUF, h, start:end], start=(b == 0), stop=(b == T * j + T - 1))
                    if end == CH:
                        mm.then_inc(pv_done, 1)

            def body(i, dn, j, final):
                last = T * j + T
                for b in range(last):
                    x = key_blocks(0, j, b)
                    aheads = (0, 1) if exists(i, dn + 1) else (0,)
                    units = [(ahead, u) for ahead in aheads for u in unit_slots.get(x - SLOTS * ahead, [])]
                    turns = [(ahead, m) for ahead, m in due(turn_slots, x) if ahead in aheads]

                    def some(quarter):
                        for ahead, u in units[len(units) * quarter // 4:len(units) * (quarter + 1) // 4]:
                            find(i, dn + ahead, u)

                    some(0)
                    scores(i, dn, j, b, 0)
                    some(1)
                    scores(i, dn, j, b, 1)
                    some(2)
                    for ahead, m in turns:
                        turn_max(i, dn + ahead, m)
                    for half in range(2):
                        if b >= 2:
                            products(i, dn, j, b - 2, half)
                        elif (dn, j) != (0, 0):
                            pdn, pj = preceding(dn, j)
                            products(i, pdn, pj, T * pj + T - 2 + b, half)
                        if half == 0:
                            some(3)
                    if b == SUM and (dn, j) != (0, 0):
                        turn_sum(i, *preceding(dn, j))
                if final:
                    for b in (last - 2, last - 1):
                        for half in range(2):
                            products(i, dn, j, b, half)
                    turn_sum(i, dn, j, True)

            pe.wait_ge(const_ok, 2)
            pe.wait_ge(ones_ok, 6)
            for x in range(MAX_FROM, 0):
                for u in unit_slots[x]:
                    find(0, 0, u)
                if x in turn_slots:
                    turn_max(0, 0, turn_slots[x])
            steps(pe, body)


def build(nc, x, w, out):
    x1 = nc.dram_tensor("x1", (TOK, E), F32, kind="Internal").ap()
    v = nc.dram_tensor("v_tok", (TOK, E), F32, kind="Internal").ap()
    qkT = nc.dram_tensor("qkT_parts", (3, 2 * E, TOK), BF16, kind="Internal").ap()
    attn = nc.dram_tensor("attn_tok", (TOK, E), F32, kind="Internal").ap()
    x2 = nc.dram_tensor("x2_tok", (TOK, E), F32, kind="Internal").ap()
    with ExitStack() as ctx:
        shared = [ctx.enter_context(nc.sbuf_tensor(name, shape, F32R)) for name, shape in
                  (("up_hi", [P, EC, F]), ("up_lo", [P, EC, F]), ("down_hi", [P, FC, E]), ("down_lo", [P, FC, E]))]
        ffn_phase(nc, True, x, x1, w, {"v": v, "qkT": qkT}, shared)
        attention_phase(nc, w, {"v": v, "qkT": qkT, "attn": attn})
        ffn_phase(nc, False, x1, out, w, {"attn": attn, "x2": x2}, shared)


def kernel(L0_attn_x, L0_attn_Wq, L0_attn_Wk, L0_attn_Wv, L0_attn_bv, L0_attn_Wo, L0_attn_bo, L0_ffn_W_fc,
           L0_ffn_W_proj):
    import numpy as np
    import concourse.bacc as bacc
    from concourse.bass_utils import run_bass_kernel_spmd

    f32 = np.float32
    inv = (f32(1.0) / f32(10000.0) ** (np.arange(0, D, 2, dtype=f32) / f32(D))).astype(f32)
    angle = np.arange(S, dtype=f32)[:, None] * inv[None, :]
    scale = f32(D ** -0.5)

    def table(t):
        return np.tile(np.concatenate([t * scale, t], axis=1).astype(f32), (B, 1))

    arrays = {
        "x": np.asarray(L0_attn_x).reshape(TOK, E),
        "up": np.asarray(L0_ffn_W_fc).T,
        "down": np.asarray(L0_ffn_W_proj).T,
        "qkv": np.concatenate([np.asarray(L0_attn_Wq).T, np.asarray(L0_attn_Wk).T, np.asarray(L0_attn_Wv).T], axis=1),
        "o": np.asarray(L0_attn_Wo).T,
        "bv": np.asarray(L0_attn_bv),
        "bo": np.asarray(L0_attn_bo),
        "cos": table(np.cos(angle)),
        "sin": table(np.sin(angle)),
        "ident": np.eye(P, dtype=f32),
        "mask": np.triu(np.full((P, P), NEG, dtype=f32), k=1),
    }
    arrays = {k: np.ascontiguousarray(a) for k, a in arrays.items()}
    nc = bacc.Bacc("TRN2", target_bir_lowering=False, num_devices=1)
    w = {k: nc.dram_tensor(f"in_{k}", a.shape, F32, kind="ExternalInput").ap() for k, a in arrays.items()}
    out = nc.dram_tensor("out", (TOK, E), F32, kind="ExternalOutput").ap()
    build(nc, w["x"], w, out)
    r = run_bass_kernel_spmd(nc, [{f"in_{k}": a for k, a in arrays.items()}], core_ids=[0])
    return r.results[0]["out"].reshape(B, S, E)
```
